# Optimizing a Trainium2 kernel written in Bass

```python
import numpy as np
import jax
import jax.numpy as jnp

def _softmax(x, axis=-1):
    return jax.nn.softmax(x, axis=axis)

def _gelu(x):
    return jax.nn.gelu(x, approximate=True)

def _silu(x):
    return jax.nn.silu(x)

def _sigmoid(x):
    return jax.nn.sigmoid(x)

def _layernorm(x, axis=-1, eps=1e-05):
    m = jnp.mean(x, axis=axis, keepdims=True)
    v = jnp.var(x, axis=axis, keepdims=True)
    return (x - m) / jnp.sqrt(v + eps)

def _scatter_add(tgt, idx, src, axis=0):
    return tgt.at[idx].add(src)

def _segment_sum(src, seg, n):
    return jax.ops.segment_sum(src, seg, n)
kernel_name = 'mk_flamingo_gated_d2_seqx_r8_72f58e'

def setup_inputs(seed: int=0):
    np.random.seed(seed)
    _w = jnp.asarray

    def _rec_inputs():
        import jax
        import jax.numpy as jnp
        _rk = jax.random.key(seed)
        x = -0.000125 + 0.9999 * jax.random.normal(jax.random.fold_in(_rk, 1), (8, 128, 512), jnp.float32)
        _lenS = 128 - jax.random.randint(jax.random.fold_in(_rk, 7), (8,), 0, max(1, 128 // 4) + 1, jnp.int32)
        _lenS2 = 128 - jax.random.randint(jax.random.fold_in(_rk, 8), (8,), 0, max(1, 128 // 4) + 1, jnp.int32)
        _ctx_4096P = jax.random.normal(jax.random.fold_in(_rk, 11), (8, 16, 512), jnp.float32)
        _ctx_4096c = jax.random.dirichlet(jax.random.fold_in(_rk, 511), 0.3 * jnp.ones((16,), jnp.float32), (8, 128))
        _ctx_4096t = jnp.einsum('bsk,bkd->bsd', _ctx_4096c, _ctx_4096P)
        _ctx_4096t = _ctx_4096t * jax.lax.rsqrt(jnp.mean(jnp.square(_ctx_4096t)) + 1e-12) * 0.953939
        ctx_4096 = -1.52775e-05 + 0.999936 * (_ctx_4096t + 0.3 * jax.random.normal(jax.random.fold_in(_rk, 611), (8, 128, 512), jnp.float32))
        _validS = jnp.arange(128)[None, :] < _lenS[:, None]
        _validS2 = jnp.arange(128)[None, :] < _lenS2[:, None]
        _causal = jnp.tril(jnp.ones((128, 128), dtype=bool))
        mask_SxS2_bk0 = jnp.logical_not(jnp.broadcast_to(_validS2[0:1, :], (128, 128)))
        _g = jax.random.normal(jax.random.fold_in(_rk, 9001), (2, 2), jnp.float32)
        _g = jnp.sign(_g) * jnp.maximum(jnp.abs(_g), 1.0) + (_g == 0) * 1.0
        g_xattn = _g[0]
        g_ffn = _g[1]
        return (x, ctx_4096, mask_SxS2_bk0, g_xattn, g_ffn)
    x, ctx_4096, mask_SxS2_bk0, g_xattn, g_ffn = _rec_inputs()

    def _L0_xattn_setup():
        import jax, jax.numpy as jnp
        import numpy as np
        H = 8
        C = 2

        def _autocorrelation(Q, K, V):
            B, L, D = Q.shape
            d = D // H
            q = Q.reshape(B, L, H, d).transpose(0, 2, 1, 3)
            k = K.reshape(B, L, H, d).transpose(0, 2, 1, 3)
            v = V.reshape(B, L, H, d).transpose(0, 2, 1, 3)
            qf = jnp.fft.fft(q, axis=2)
            kf = jnp.fft.fft(k, axis=2)
            corr = jnp.fft.ifft(qf * jnp.conj(kf), axis=2).real
            topk = int(C * np.log(L))
            w, idx = jax.lax.top_k(corr.transpose(0, 1, 3, 2), topk)
            w = jax.nn.softmax(w, axis=-1)
            pos = jnp.arange(L)[:, None]
            out = jnp.zeros_like(v)
            for i in range(topk):
                g = jnp.minimum(idx[:, :, None, :, i] + pos, L - 1)
                out = out + w[:, :, None, :, i] * jnp.take_along_axis(v, g, axis=2)
            return out.transpose(0, 2, 1, 3).reshape(B, L, D)
        key = jax.random.key(seed)
        k1, k2, k3 = jax.random.split(key, 3)
        B, L, D = (16, 64, 512)
        Q = jax.random.normal(k1, (B, L, D), dtype=jnp.float32)
        K = jax.random.normal(k2, (B, L, D), dtype=jnp.float32)
        V = jax.random.normal(k3, (B, L, D), dtype=jnp.float32)
        return {'Q': Q, 'K': K, 'V': V}
    _L0_xattn_all = _L0_xattn_setup()
    _L0_xattn_in = {k: v for k, v in _L0_xattn_all.items() if k in ()}
    del _L0_xattn_all

    def _L0_ffn_setup():
        import jax, jax.numpy as jnp
        import numpy as np
        B_, S, D_IN, D_OUT = (4, 256, 512, 512)
        N, RANK, ALPHA = (8, 16, 32)
        SCALE = ALPHA / RANK
        key = jax.random.key(seed)
        kx, ka, kb, kw, kbias = jax.random.split(key, 5)
        x = jax.random.normal(kx, (B_, S, D_IN), dtype=jnp.float32)
        lora_A = jax.random.normal(ka, (N, RANK, D_IN), dtype=jnp.float32) * (1.0 / np.sqrt(D_IN))
        lora_B = jax.random.normal(kb, (N, D_OUT, RANK), dtype=jnp.float32) * (1.0 / np.sqrt(RANK))
        W = jax.random.normal(kw, (D_OUT, D_IN), dtype=jnp.float32) * (1.0 / np.sqrt(D_IN))
        bias = jax.random.normal(kbias, (D_OUT,), dtype=jnp.float32) * 0.01
        lora_weights = jnp.full((N,), 1.0 / N, dtype=jnp.float32)
        return {'x': x, 'lora_A': lora_A, 'lora_B': lora_B, 'W': W, 'bias': bias, 'lora_weights': lora_weights}
    _L0_ffn_all = _L0_ffn_setup()
    _L0_ffn_in = {k: v for k, v in _L0_ffn_all.items() if k in ('lora_A', 'lora_B', 'W', 'bias', 'lora_weights')}
    del _L0_ffn_all

    def _L1_xattn_setup():
        import jax, jax.numpy as jnp
        import numpy as np
        N_HEAD = 32
        D_MODEL = 512
        N_KV_GROUPS = 8
        D_HEAD = D_MODEL // N_HEAD
        H_PER_G = N_HEAD // N_KV_GROUPS
        KV_DIM = N_KV_GROUPS * D_HEAD
        B, S = (2, 256)
        key = jax.random.key(seed)
        ks = jax.random.split(key, 8)
        q = jax.random.normal(ks[0], (B, S, D_MODEL), dtype=jnp.float32)
        k = jax.random.normal(ks[1], (B, S, D_MODEL), dtype=jnp.float32)
        v = jax.random.normal(ks[2], (B, S, D_MODEL), dtype=jnp.float32)
        mask = jnp.tril(jnp.ones((S, S), dtype=bool))
        w_q = jax.random.uniform(ks[3], (D_MODEL, D_MODEL), dtype=jnp.float32) * 0.02
        w_k = jax.random.uniform(ks[4], (KV_DIM, D_MODEL), dtype=jnp.float32) * 0.02
        w_v = jax.random.uniform(ks[5], (KV_DIM, D_MODEL), dtype=jnp.float32) * 0.02
        w_out = jax.random.uniform(ks[6], (D_MODEL, D_MODEL), dtype=jnp.float32) * 0.02
        return {'q': q, 'k': k, 'v': v, 'w_q': w_q, 'w_k': w_k, 'w_v': w_v, 'w_out': w_out, 'mask': mask}
    _L1_xattn_all = _L1_xattn_setup()
    _L1_xattn_in = {k: v for k, v in _L1_xattn_all.items() if k in ('w_q', 'w_k', 'w_v', 'w_out')}
    del _L1_xattn_all

    def _L1_ffn_setup():
        import jax, jax.numpy as jnp
        import numpy as np
        BATCH, SEQ, D = (2, 256, 512)
        K, TOPK, RANK = (64, 16, 16)
        ALPHA = 32.0
        SCALING = ALPHA / RANK
        key = jax.random.key(seed)
        k1, k2, k3, k4 = jax.random.split(key, 4)
        x = jax.random.normal(k1, (BATCH, SEQ, D), dtype=jnp.float32)
        A = jax.random.normal(k2, (K, RANK, D), dtype=jnp.float32) * 0.02
        B = jax.random.normal(k3, (K, D, RANK), dtype=jnp.float32) * 0.02
        Wr = jax.random.normal(k4, (K, D), dtype=jnp.float32) * 0.02
        return {'x': x, 'A': A, 'B': B, 'Wr': Wr}
    _L1_ffn_all = _L1_ffn_setup()
    _L1_ffn_in = {k: v for k, v in _L1_ffn_all.items() if k in ('A', 'B', 'Wr')}
    del _L1_ffn_all
    return {'x': x, 'ctx_4096': ctx_4096, 'mask_SxS2_bk0': mask_SxS2_bk0, 'g_xattn': g_xattn, 'g_ffn': g_ffn, 'L0_ffn_lora_A': _L0_ffn_in['lora_A'], 'L0_ffn_lora_B': _L0_ffn_in['lora_B'], 'L0_ffn_W': _L0_ffn_in['W'], 'L0_ffn_bias': _L0_ffn_in['bias'], 'L0_ffn_lora_weights': _L0_ffn_in['lora_weights'], 'L1_xattn_w_q': _L1_xattn_in['w_q'], 'L1_xattn_w_k': _L1_xattn_in['w_k'], 'L1_xattn_w_v': _L1_xattn_in['w_v'], 'L1_xattn_w_out': _L1_xattn_in['w_out'], 'L1_ffn_A': _L1_ffn_in['A'], 'L1_ffn_B': _L1_ffn_in['B'], 'L1_ffn_Wr': _L1_ffn_in['Wr']}

def reference(x, ctx_4096, mask_SxS2_bk0, g_xattn, g_ffn, L0_ffn_lora_A, L0_ffn_lora_B, L0_ffn_W, L0_ffn_bias, L0_ffn_lora_weights, L1_xattn_w_q, L1_xattn_w_k, L1_xattn_w_v, L1_xattn_w_out, L1_ffn_A, L1_ffn_B, L1_ffn_Wr):
    import jax
    import jax.numpy as jnp

    def _L0_xattn_ref(Q, K, V):
        import jax, jax.numpy as jnp
        import numpy as np
        H = 8
        C = 2

        def _autocorrelation(Q, K, V):
            B, L, D = Q.shape
            d = D // H
            q = Q.reshape(B, L, H, d).transpose(0, 2, 1, 3)
            k = K.reshape(B, L, H, d).transpose(0, 2, 1, 3)
            v = V.reshape(B, L, H, d).transpose(0, 2, 1, 3)
            qf = jnp.fft.fft(q, axis=2)
            kf = jnp.fft.fft(k, axis=2)
            corr = jnp.fft.ifft(qf * jnp.conj(kf), axis=2).real
            topk = int(C * np.log(L))
            w, idx = jax.lax.top_k(corr.transpose(0, 1, 3, 2), topk)
            w = jax.nn.softmax(w, axis=-1)
            pos = jnp.arange(L)[:, None]
            out = jnp.zeros_like(v)
            for i in range(topk):
                g = jnp.minimum(idx[:, :, None, :, i] + pos, L - 1)
                out = out + w[:, :, None, :, i] * jnp.take_along_axis(v, g, axis=2)
            return out.transpose(0, 2, 1, 3).reshape(B, L, D)
        return _autocorrelation(Q, K, V)

    def _L0_ffn_ref(x, lora_A, lora_B, W, bias, lora_weights):
        import jax, jax.numpy as jnp
        import numpy as np
        B_, S, D_IN, D_OUT = (4, 256, 512, 512)
        N, RANK, ALPHA = (8, 16, 32)
        SCALE = ALPHA / RANK
        h = jnp.einsum('bsd,nrd->nbsr', x, lora_A)
        coef = (SCALE * lora_weights)[:, None, None]
        lora_out = jnp.einsum('nbsr,nor->bso', h, lora_B * coef)
        base = jnp.einsum('bsd,od->bso', x, W) + bias
        return base + lora_out

    def _L1_xattn_ref(q, k, v, w_q, w_k, w_v, w_out, mask):
        import jax, jax.numpy as jnp
        import numpy as np
        N_HEAD = 32
        D_MODEL = 512
        N_KV_GROUPS = 8
        D_HEAD = D_MODEL // N_HEAD
        H_PER_G = N_HEAD // N_KV_GROUPS
        KV_DIM = N_KV_GROUPS * D_HEAD
        B, S = (2, 256)
        b, n, _ = q.shape
        s = k.shape[1]
        query = q @ w_q.T
        key = k @ w_k.T
        value = v @ w_v.T
        query = query.reshape(b, n, N_HEAD, D_HEAD).transpose(0, 2, 1, 3)
        query = query.reshape(b, N_KV_GROUPS, H_PER_G, n, D_HEAD)
        key = key.reshape(b, s, N_KV_GROUPS, D_HEAD).transpose(0, 2, 1, 3)
        value = value.reshape(b, s, N_KV_GROUPS, D_HEAD).transpose(0, 2, 1, 3)
        scores = jnp.einsum('bghnd,bgsd->bghns', query, key) / D_HEAD ** 0.5
        scores = jnp.where(mask, scores, jnp.finfo(scores.dtype).min)
        attention = jax.nn.softmax(scores, axis=-1)
        out = jnp.einsum('bghns,bgsd->bghnd', attention, value)
        out = out.transpose(0, 3, 1, 2, 4).reshape(b, n, D_MODEL)
        return out @ w_out.T

    def _L1_ffn_ref(x, A, B, Wr):
        import jax, jax.numpy as jnp
        import numpy as np
        BATCH, SEQ, D = (2, 256, 512)
        K, TOPK, RANK = (64, 16, 16)
        ALPHA = 32.0
        SCALING = ALPHA / RANK
        prefix = x.shape[:-1]
        xf = x.reshape(-1, x.shape[-1])
        N = xf.shape[0]
        scores = xf @ Wr.T
        top_vals, top_idx = jax.lax.top_k(scores, TOPK)
        gates = jax.nn.softmax(top_vals, axis=-1)
        G = jnp.zeros((N, K), xf.dtype).at[jnp.arange(N)[:, None], top_idx].set(gates)
        h = jnp.einsum('nd,krd->nkr', xf, A)
        out = jnp.einsum('nkr,kdr->nd', h * G[:, :, None], B)
        return (out * SCALING).reshape(*prefix, -1)
    x = x + jnp.tanh(g_xattn[0]) * _L0_xattn_ref(_layernorm(x, axis=-1), ctx_4096, ctx_4096)
    x = x + jnp.tanh(g_ffn[0]) * _L0_ffn_ref(_layernorm(x, axis=-1), L0_ffn_lora_A, L0_ffn_lora_B, L0_ffn_W, L0_ffn_bias, L0_ffn_lora_weights)
    x = x + jnp.tanh(g_xattn[1]) * _L1_xattn_ref(_layernorm(x, axis=-1), ctx_4096, ctx_4096, L1_xattn_w_q, L1_xattn_w_k, L1_xattn_w_v, L1_xattn_w_out, mask_SxS2_bk0)
    x = x + jnp.tanh(g_ffn[1]) * _L1_ffn_ref(_layernorm(x, axis=-1), L1_ffn_A, L1_ffn_B, L1_ffn_Wr)
    return x

_drawn_inputs = setup_inputs


def setup_inputs(seed=0):
    import zlib

    import numpy as np

    out = dict(_drawn_inputs(seed))
    spreads = {'g_ffn': (-1.0, 0.6), 'L0_ffn_lora_weights': (0.125, 0.2)}
    factors = {'L0_ffn_bias': 8.0,
     'L1_xattn_w_out': 6.541,
     'L1_ffn_A': 5.874,
     'L1_ffn_B': 5.633,
     'L1_ffn_Wr': 6.512}
    for name, (base, spread) in spreads.items():
        noise = np.random.default_rng([zlib.crc32(name.encode()), seed]).standard_normal(out[name].shape)
        drawn = base * np.exp(spread * noise) if base else spread * noise
        out[name] = jnp.asarray(drawn.astype(out[name].dtype))
    for name, factor in factors.items():
        out[name] = (out[name] * factor).astype(out[name].dtype)
    return out
```

```python
from contextlib import ExitStack

import numpy as np

import concourse.bass as bass
from concourse import mybir

F32 = mybir.dt.float32
BF16 = mybir.dt.bfloat16
ALU = mybir.AluOpType
ACT = mybir.ActivationFunctionType
AX = mybir.AxisListType.X

B, S, D = 8, 128, 512
P = 128
C = D // P
PAIRS = B // 2
EPS = 1e-5

DELAYS = 9
TAKEN = -2.0 ** 127
STAND_IN = -1.5 * 2.0 ** 127
FILL = 7

HEADS, GROUPS, DH = 32, 8, 16
HPG = HEADS // GROUPS
QUADS = 8
VW = DH + 1

EXPERTS, TOPK, RANK = 64, 16, 16
KR = EXPERTS * RANK
KC = KR // P

MATS = ["FA", "FB2", "FC1", "FC2", "FO", "G1", "G2", "H1", "H2", "J1", "J2", "ID"]


def transform_matrices():
    t = np.arange(S)
    r = np.arange(S)
    re = r <= S // 2
    k = np.where(re, r, r - S // 2)
    a = 2 * np.pi * np.outer(k, t) / S
    cos, sin = np.cos(a), np.sin(a)
    fa = np.where(re[:, None], cos, -sin)
    fb2 = -sin.copy()
    fb2[0, :] = t == S - 1
    w = np.where((k == 0) | (k == S // 2), 1.0, 2.0)[:, None] / S
    g1 = np.where(re[:, None], w * cos, -w * sin)
    g2 = np.where(re[:, None], w * sin, w * cos)
    h1 = 0.5 * np.where(re[:, None], w * cos, w * sin)
    h2 = 0.5 * np.where(re[:, None], -w * sin, w * cos)
    h2[0, :] = 0.5
    hr = r < S // 2
    kk = np.where(hr, r, r - S // 2) + 0.5
    o = 2 * np.pi * np.outer(kk, t) / S
    oc, os = np.cos(o), np.sin(o)
    less_last = np.eye(S)
    less_last[:, S - 1] -= 1.0
    fo = np.where(hr[:, None], oc, -os)
    j1 = (1.0 / S) * np.where(hr[:, None], oc, os)
    j2 = (1.0 / S) * np.where(hr[:, None], -os, oc)
    fb1 = cos
    mats = {"FA": fa.T, "FB1": fb1.T, "FB2": fb2.T, "FC1": (oc @ less_last).T, "FC2": (-os @ less_last).T,
            "FO": fo.T, "G1": g1, "G2": g2, "H1": h1, "H2": h2, "J1": j1, "J2": j2, "ID": np.eye(S)}
    return mats


MATS = list(transform_matrices())


def flamingo_kernel(nc, x, ctx_in, mask, gates, w_base, lora_a, lora_b, lora_w, bias, wq, wk, wv, wo,
                    moe_a, moe_b, w_router, mats, parity, out):
    with ExitStack() as st:
        def sb(name, shape, dt=F32):
            return st.enter_context(nc.sbuf_tensor(name, shape, dt))

        def sem(name):
            return st.enter_context(nc.semaphore(name))

        def sems(name):
            return [sem(f"{name}{u}") for u in (0, 1)]

        X = sb("X", [P, B, D])
        stats = sb("stats", [P, B, 2])
        rstd = sb("rstd", [P, B])
        M = sb("M", [P, len(MATS), S])
        mat = {n: M[:, k, :] for k, n in enumerate(MATS)}
        ident = mat["ID"]
        ident_bf = sb("ident_bf", [P, P], BF16)
        mask_u8 = sb("mask_u8", [P, S], mybir.dt.uint8)
        never = sb("never", [P, S], BF16)
        par = sb("par", [P, 2])
        g_in = sb("g_in", [P, 4])
        tg = sb("tg", [P, 4])
        W0 = sb("W0", [P, C, D])
        LA = sb("LA", [P, D])
        LB = sb("LB", [P, D])
        lw = sb("lw", [P, 2])
        BI = sb("BI", [P, D])
        WQ = sb("WQ", [P, C, D])
        WK = sb("WK", [P, C, P])
        WV = sb("WV", [P, C, P])
        WO = sb("WO", [P, C, D])
        MA = sb("MA", [P, C, KR])
        MB = sb("MB", [P, KC, D])
        WR = sb("WR", [P, C, EXPERTS])
        zero_eps = sb("zero_eps", [P, 2])
        neg_half = sb("neg_half", [P, 1])

        ctx_s = sb("ctx_s", [P, 2, D])
        xn = sb("xn", [P, 2, D])
        bn = sb("bn", [P, 2, 6])
        mv = sb("mv", [P, 2, 2])
        tick = sb("tick", [P, 1])
        xT = sb("xT", [P, 2, C, P])
        big = sb("big", [P, 2, 8, D])
        small = sb("small", [P, 2, 256])

        bank = st.enter_context(nc.psum_tensor("bank", [P, 8, D], F32))

        x_in, ctx_ld = sems("x_in"), sems("ctx_ld")
        mats_in, gate_in, mask_in = sem("mats_in"), sem("gate_in"), sem("mask_in")
        lora_in, attn_in, moe_in = sem("lora_in"), sem("attn_in"), sem("moe_in")
        consts_set, tanh_done, scaled = sem("consts_set"), sem("tanh_done"), sem("scaled")
        ready_bf = sem("ready_bf")
        bn_done = [sem(f"bn_done{p}") for p in range(4)]
        mv_done = [sem(f"mv_done{p}") for p in range(4)]
        stats_done = [sem(f"stats_done{p}") for p in range(4)]
        rstd_done = [sem(f"rstd_done{p}") for p in range(4)]
        normed = [sem(f"normed{p}") for p in range(4)]
        x_new = [sems(f"x_new{p}_") for p in range(4)]

        b1_mm, b2_mm, a_mm, c1_mm = (sem(n) for n in ("b1_mm", "b2_mm", "a_mm", "c1_mm"))
        c2_mm, cT_mm = sems("c2_mm"), sems("cT_mm")
        b1_out, b2_out, c1_out, c2_out = (sem(n) for n in ("b1_out", "b2_out", "c1_out", "c2_out"))
        corr_prod, corr_mm = sem("corr_prod"), sem("corr_mm")
        top8, neg_top, less8, next8, ninth_set = (sem(n) for n in ("top8", "neg_top", "less8", "next8", "ninth_set"))
        less9, kept_mask, vals_sub, vals_exp = (sem(n) for n in ("less9", "kept_mask", "vals_sub", "vals_exp"))
        exp_c, vals_sum, inv_sum, w_built = (sem(n) for n in ("exp_c", "vals_sum", "inv_sum", "w_built"))
        wt_mm, wt_out, we_mm, wo_mm, spec_prod, inv_mm = (sem(n) for n in ("wt_mm", "wt_out", "we_mm", "wo_mm", "spec_prod", "inv_mm"))

        lora_mm, lora_folded = sem("lora_mm"), sem("lora_folded")
        x_bias = sem("x_bias")
        xT_mm = [sem(f"xT_mm{p}") for p in range(4)]
        xT_out = [sem(f"xT_out{p}") for p in range(4)]
        y_mm = sem("y_mm")

        cT_out, q_mm, q_out, kv_mm, kv_out = (sem(n) for n in ("cT_out", "q_mm", "q_out", "kv_mm", "kv_out"))
        score_mm, row_max, less_max, probs, pT_mm, pT_out, av_mm = (
            sem(n) for n in ("score_mm", "row_max", "less_max", "probs", "pT_mm", "pT_out", "av_mm"))
        inv_den, att_set, aT_mm, aT_out, o_mm = (sem(n) for n in ("inv_den", "att_set", "aT_mm", "aT_out", "o_mm"))

        r_mm, h_mm, r_top, r_less, r_top2, r_less2, r_neg, r_exp, r_kept, r_sum, r_inv, gate_set = (
            sem(n) for n in ("r_mm", "h_mm", "r_top", "r_less", "r_top2", "r_less2", "r_neg", "r_exp",
                             "r_kept", "r_sum", "r_inv", "gate_set"))
        hg_set, hT_mm, hT_out, e_mm, stored = (sem(n) for n in ("hg_set", "hT_mm", "hT_out", "e_mm", "stored"))

        B1s, B2s, C1s, C2s = ([big[:, u, k, :] for u in (0, 1)] for k in range(4))
        spec = [[big[:, u, 4 + k, :] for k in range(4)] for u in (0, 1)]
        less = sb("less", [P, 2, 2, C, S + FILL])
        expc = sb("expc", [P, 2, C, S])
        kept = sb("kept", [P, 2, C, S])
        wts = sb("wts", [P, 2, C, S])
        wT = sb("wT", [P, 2, D])
        top9 = sb("top9", [P, 2, C, DELAYS])
        nxt = sb("nxt", [P, 2, C, 8])
        ninth = sb("ninth", [P, 2, C, 8])
        ntop = sb("ntop", [P, 2, C])
        vals = sb("vals", [P, 2, C, DELAYS])
        vsum = sb("vsum", [P, 2, 2, C])
        cT = wT
        qT = [big[:, u, 0, :] for u in (0, 1)]
        kEO = [big[:, u, 1, 0:2 * S].rearrange("p (e s) -> p e s", e=2) for u in (0, 1)]
        vx = [big[:, u, 2, 0:GROUPS * VW].rearrange("p (g w) -> p g w", g=GROUPS) for u in (0, 1)]
        att = [big[:, u, 3, :] for u in (0, 1)]
        attT = [big[:, u, 4, :].rearrange("p (c n) -> p c n", c=C) for u in (0, 1)]
        E = [big[:, k // 3, 5 + k % 3, :].rearrange("p (h s) -> p h s", h=4) for k in range(4)]
        ET = [expc[:, k, :, :] for k in (0, 1)]
        mx = sb("mx", [P, 4, 4])
        iden = sb("iden", [P, 2, GROUPS * 2])
        hg = [big[:, u, 0:2, :].rearrange("p a (k r) -> p (a k) r", r=RANK) for u in (0, 1)]
        hT = [big[:, u, 2:4, :].rearrange("p a (c n) -> p (a c) n", n=P) for u in (0, 1)]
        rl = sb("rl", [P, 2, 2, EXPERTS])
        rt = sb("rt", [P, 2, 2, 8])
        re = sb("re", [P, 2, EXPERTS])
        rk = sb("rk", [P, 2, EXPERTS])
        G = sb("G", [P, 2, EXPERTS])
        rs = sb("rs", [P, 2, 4])

        block = st.enter_context(nc.Block())

        @block.sync
        def _(sp):
            for u in (0, 1):
                sp.sem_inc(x_in[u], 16)
                sp.sem_inc(c2_mm[u], 1)
                sp.sem_inc(cT_mm[u], 1)
                for p in range(4):
                    sp.sem_inc(x_new[p][u], 1)
            sp.dma_start(M[:], mats).then_inc(mats_in, 16)
            with sp.Fori(0, PAIRS) as i:
                for u in (0, 1):
                    sp.wait_ge(x_in[u], 16 * i + 16)
                    sp.dma_start(X[:, 2 * i + u, :], x[2 * i + u]).then_inc(x_in[u], 16)
            with sp.Fori(0, PAIRS) as i:
                for u in (0, 1):
                    sp.wait_ge(c2_mm[u], i + 1)
                    sp.dma_start(ctx_s[:, u, :], ctx_in[2 * i + u]).then_inc(ctx_ld[u], 16)
            for u in (0, 1):
                sp.wait_ge(c2_mm[u], PAIRS + 1)
            with sp.Fori(0, PAIRS) as i:
                for u in (0, 1):
                    sp.wait_ge(cT_mm[u], i + 1)
                    sp.dma_start(ctx_s[:, u, :], ctx_in[2 * i + u]).then_inc(ctx_ld[u], 16)
            with sp.Fori(0, PAIRS) as i:
                for u in (0, 1):
                    sp.wait_ge(x_new[3][u], i + 2)
                    sp.dma_start(out[2 * i + u], X[:, 2 * i + u, :]).then_inc(stored, 16)
            sp.wait_ge(stored, 16 * B)

        @block.gpsimd
        def _(pool):
            g = nc.gpsimd
            g.memset(zero_eps[:, 0:1], 0.0).then_inc(consts_set, 1)
            g.memset(zero_eps[:, 1:2], EPS).then_inc(consts_set, 1)
            g.memset(neg_half[:], -0.5).then_inc(consts_set, 1)
            g.memset(less[:], STAND_IN).then_inc(consts_set, 1)
            g.memset(ninth[:], STAND_IN).then_inc(consts_set, 1)
            pool.wait_ge(consts_set, 5)

            def inverse_std(p, b, u):
                pool.wait_ge(stats_done[p], b + 1)
                pool.wait_ge(consts_set, 5)
                g.tensor_tensor(rstd[:, bass.ds(b, 1)], stats[:, b, 1:2], neg_half[:], ALU.pow).then_inc(rstd_done[p], 1)

            with pool.Fori(0, PAIRS) as i:
                for u in (0, 1):
                    inverse_std(0, 2 * i + u, u)

            pool.wait_ge(tanh_done, 1)
            pool.wait_ge(lora_in, 16 * 5)
            g.tensor_scalar(lw[:, 1:2], lw[:, 0:1], tg[:, 1:2], 2.0, ALU.mult, ALU.mult).then_inc(scaled, 1)
            pool.wait_ge(scaled, 1)
            g.tensor_scalar(LB[:], LB[:], lw[:, 1:2], 1.0, ALU.mult, ALU.mult).then_inc(scaled, 1)
            g.tensor_scalar(W0[:], W0[:], tg[:, 1:2], 1.0, ALU.mult, ALU.mult).then_inc(scaled, 1)
            g.tensor_scalar(BI[:], BI[:], tg[:, 1:2], 1.0, ALU.mult, ALU.mult).then_inc(scaled, 1)
            pool.wait_ge(attn_in, 16 * 4)
            g.tensor_scalar(WO[:], WO[:], tg[:, 2:3], 1.0, ALU.mult, ALU.mult).then_inc(scaled, 1)
            pool.wait_ge(moe_in, 16 * 3)
            g.tensor_scalar(MB[:], MB[:], tg[:, 3:4], 2.0, ALU.mult, ALU.mult).then_inc(scaled, 1)

            with pool.Fori(0, PAIRS) as i:
                for u in (0, 1):
                    inverse_std(1, 2 * i + u, u)
            pool.wait_ge(scaled, 4)
            with pool.Fori(0, PAIRS) as i:
                for u in (0, 1):
                    pool.wait_ge(x_new[1][u], i + 1)
                    pool.wait_ge(x_new[0][1], PAIRS + 1)
                    g.tensor_tensor(big[:, u, 0, :], X[:, 2 * i + u, :], BI[:], ALU.add).then_inc(x_bias, 1)
                for u in (0, 1):
                    inverse_std(2, 2 * i + u, u)
            with pool.Fori(0, PAIRS) as i:
                for u in (0, 1):
                    inverse_std(3, 2 * i + u, u)

        @block.scalar
        def _(act):
            a = nc.scalar
            act.dma_start(g_in[:], gates).then_inc(gate_in, 16)
            act.dma_start(mask_u8[:], mask).then_inc(mask_in, 16)
            act.dma_start(par[:], parity).then_inc(mask_in, 16)
            act.dma_start(W0[:], w_base).then_inc(lora_in, 16)
            act.dma_start(LA[:], lora_a).then_inc(lora_in, 16)
            act.dma_start(LB[:], lora_b).then_inc(lora_in, 16)
            act.dma_start(lw[:, 0:1], lora_w).then_inc(lora_in, 16)
            act.dma_start(BI[:], bias).then_inc(lora_in, 16)
            act.dma_start(WQ[:], wq).then_inc(attn_in, 16)
            act.dma_start(WK[:], wk).then_inc(attn_in, 16)
            act.dma_start(WV[:], wv).then_inc(attn_in, 16)
            act.dma_start(WO[:], wo).then_inc(attn_in, 16)
            act.dma_start(MA[:], moe_a).then_inc(moe_in, 16)
            act.dma_start(MB[:], moe_b).then_inc(moe_in, 16)
            act.dma_start(WR[:], w_router).then_inc(moe_in, 16)
            act.wait_ge(gate_in, 16)
            a.activation(tg[:], g_in[:], ACT.Tanh).then_inc(tanh_done, 1)

            def copy(dst, src):
                return a.activation(dst, src, ACT.Copy)

            with act.Fori(0, PAIRS) as i:
                for u in (0, 1):
                    b, k = 2 * i + u, 4 * u
                    act.wait_ge(b1_mm, b + 1)
                    copy(B1s[u], bank[:, k + 0, :]).then_inc(b1_out, 1)
                    act.wait_ge(b2_mm, b + 1)
                    copy(B2s[u], bank[:, k + 1, :]).then_inc(b2_out, 1)
                    act.wait_ge(c1_mm, b + 1)
                    copy(C1s[u], bank[:, k + 3, :]).then_inc(c1_out, 1)
                    act.wait_ge(c2_mm[u], i + 2)
                    copy(C2s[u], bank[:, k + 0, :]).then_inc(c2_out, 1)
                for u in (0, 1):
                    b, k = 2 * i + u, 4 * u
                    act.wait_ge(neg_top, b + 1)
                    act.wait_ge(less8, C * b + C)
                    for c in range(C):
                        a.activation(expc[:, u, c, :], bank[:, k + 1, c * S:(c + 1) * S], ACT.Exp,
                                     bias=ntop[:, u, c:c + 1]).then_inc(exp_c, 1)
                    act.wait_ge(vals_sub, b + 1)
                    a.activation(vals[:, u, :, :], vals[:, u, :, :], ACT.Exp).then_inc(vals_exp, 1)
                for u in (0, 1):
                    b, k = 2 * i + u, 4 * u
                    act.wait_ge(wt_mm, b + 1)
                    copy(wT[:, u, :], bank[:, k + 2, :]).then_inc(wt_out, 1)

            with act.Fori(0, PAIRS) as i:
                for u in (0, 1):
                    act.wait_ge(xT_mm[1], 2 * i + u + 1)
                    copy(xT[:, u, :, :], bank[:, 4 * u, :]).then_inc(xT_out[1], 1)

            with act.Fori(0, PAIRS) as i:
                for u in (0, 1):
                    b = 2 * i + u
                    act.wait_ge(xT_mm[2], b + 1)
                    copy(xT[:, u, :, :], bank[:, 4, :]).then_inc(xT_out[2], 1)
                    act.wait_ge(q_mm, b + 1)
                    copy(qT[u], bank[:, 0, :]).then_inc(q_out, 1)
                    for k in range(QUADS + 1):
                        if k < QUADS:
                            act.wait_ge(less_max, QUADS * b + k + 1)
                            a.activation(E[k % 4], E[k % 4], ACT.Exp, scale=DH ** -0.5).then_inc(probs, 1)
                        if k > 0:
                            if k >= 3:
                                act.wait_ge(av_mm, QUADS * b + k - 2)
                            act.wait_ge(pT_mm, QUADS * b + k)
                            copy(ET[(k - 1) % 2], bank[:, 4 + (k - 1) % 2, :]).then_inc(pT_out, 1)
                    act.wait_ge(aT_mm, b + 1)
                    copy(attT[u], bank[:, 4, :]).then_inc(aT_out, 1)

            with act.Fori(0, PAIRS) as i:
                for u in (0, 1):
                    b = 2 * i + u
                    act.wait_ge(xT_mm[3], b + 1)
                    copy(xT[:, u, :, :], bank[:, 4 * u, :]).then_inc(xT_out[3], 1)
                for u in (0, 1):
                    b = 2 * i + u
                    act.wait_ge(r_neg, b + 1)
                    act.wait_ge(r_less, b + 1)
                    a.activation(re[:, u, :], bank[:, 4 * u + 1, 0:EXPERTS], ACT.Exp, bias=rs[:, u, 0:1]).then_inc(r_exp, 1)
                for u in (0, 1):
                    for v in (0, 1):
                        act.wait_ge(hT_mm, 4 * i + 2 * u + v + 1)
                        copy(hT[u][:, 4 * v:4 * v + 4, :], bank[:, 4 * u + v, :]).then_inc(hT_out, 1)

        @block.vector
        def _(dve):
            v = nc.vector

            def settle():
                v.memset(tick[:], 0.0)

            def token_stats(p, b, u):
                settle()
                v.bn_stats(bn[:, u, :], X[:, b, :]).then_inc(bn_done[p], 1)
                dve.wait_ge(bn_done[p], b + 1)
                settle()
                v.bn_aggr(mv[:, u, :], bn[:, u, :]).then_inc(mv_done[p], 1)
                dve.wait_ge(mv_done[p], b + 1)
                v.tensor_tensor(stats[:, b, :], mv[:, u, :], zero_eps[:], ALU.add).then_inc(stats_done[p], 1)

            def normalise(p, b, u):
                dve.wait_ge(rstd_done[p], b + 1)
                v.tensor_scalar(xn[:, u, :], X[:, b, :], stats[:, b, 0:1], rstd[:, bass.ds(b, 1)],
                                ALU.subtract, ALU.mult).then_inc(normed[p], 1)

            dve.wait_ge(consts_set, 5)
            with dve.Fori(0, PAIRS) as i:
                for u in (0, 1):
                    dve.wait_ge(x_in[u], 16 * i + 32)
                    token_stats(0, 2 * i + u, u)
            dve.wait_ge(mats_in, 16)
            v.tensor_copy(ident_bf[:], ident).then_inc(ready_bf, 1)
            dve.wait_ge(mask_in, 32)
            v.tensor_scalar(never[:], mask_u8[:], 0.0, TAKEN, ALU.is_equal, ALU.mult).then_inc(ready_bf, 1)

            def correlation_products(b, u):
                k = 4 * u
                dve.wait_ge(a_mm, b + 1)
                dve.wait_ge(b1_out, b + 1)
                v.tensor_tensor(spec[u][0], bank[:, k + 2, :], B1s[u], ALU.mult).then_inc(corr_prod, 1)
                dve.wait_ge(b2_out, b + 1)
                v.tensor_tensor(spec[u][1], bank[:, k + 2, :], B2s[u], ALU.mult).then_inc(corr_prod, 1)

            def pick_nine(b, u):
                corr = bank[:, 4 * u + 1, :].rearrange("p (c s) -> p c s", c=C)
                dve.wait_ge(corr_mm, b + 1)
                settle()
                for c in range(C):
                    v.max(top9[:, u, c, 0:8], corr[:, c, :]).then_inc(top8, 1)
                dve.wait_ge(top8, C * b + C)
                v.tensor_scalar(ntop[:, u, :], top9[:, u, :, 0], -1.0, None, ALU.mult).then_inc(neg_top, 1)
                for c in range(C):
                    v.match_replace(less[:, u, 0, c, 0:S], top9[:, u, c, 0:8], corr[:, c, :], TAKEN).then_inc(less8, 1)
                dve.wait_ge(less8, C * b + C)
                settle()
                for c in range(C):
                    v.max(nxt[:, u, c, :], less[:, u, 0, c, 0:S]).then_inc(next8, 1)
                dve.wait_ge(next8, C * b + C)
                v.tensor_copy(ninth[:, u, :, 0], nxt[:, u, :, 0]).then_inc(ninth_set, 1)
                v.tensor_copy(top9[:, u, :, 8], nxt[:, u, :, 0]).then_inc(ninth_set, 1)
                dve.wait_ge(ninth_set, 2 * b + 2)
                v.tensor_tensor(vals[:, u, :, :], top9[:, u, :, :],
                                ntop[:, u, :].unsqueeze(2).broadcast_to([P, C, DELAYS]), ALU.add).then_inc(vals_sub, 1)
                for c in range(C):
                    v.match_replace(less[:, u, 1, c, :], ninth[:, u, c, :], less[:, u, 0, c, :], TAKEN).then_inc(less9, 1)
                dve.wait_ge(less9, C * b + C)
                v.tensor_scalar(kept[:, u, :, :], less[:, u, 1, :, 0:S], TAKEN, None, ALU.is_equal).then_inc(kept_mask, 1)
                dve.wait_ge(vals_exp, b + 1)
                v.reduce_sum(vsum[:, u, 0, :], vals[:, u, :, :], AX).then_inc(vals_sum, 1)
                dve.wait_ge(vals_sum, b + 1)
                v.reciprocal(vsum[:, u, 1, :], vsum[:, u, 0, :]).then_inc(inv_sum, 1)
                dve.wait_ge(inv_sum, b + 1)
                dve.wait_ge(kept_mask, b + 1)
                dve.wait_ge(exp_c, C * b + C)
                for c in range(C):
                    v.scalar_tensor_tensor(wts[:, u, c, :], expc[:, u, c, :], vsum[:, u, 1, c:c + 1],
                                           kept[:, u, c, :], ALU.mult, ALU.mult).then_inc(w_built, 1)

            def delay_products(b, u):
                k = 4 * u
                dve.wait_ge(we_mm, b + 1)
                v.tensor_tensor(spec[u][0], bank[:, k + 3, :], B1s[u], ALU.mult).then_inc(spec_prod, 1)
                v.tensor_tensor(spec[u][1], bank[:, k + 3, :], B2s[u], ALU.mult).then_inc(spec_prod, 1)
                dve.wait_ge(wo_mm, b + 1)
                v.tensor_tensor(spec[u][2], bank[:, k + 1, :], C1s[u], ALU.mult).then_inc(spec_prod, 1)
                v.tensor_tensor(spec[u][3], bank[:, k + 1, :], C2s[u], ALU.mult).then_inc(spec_prod, 1)

            with dve.Fori(0, PAIRS) as i:
                for u in (0, 1):
                    normalise(0, 2 * i + u, u)
                for u in (0, 1):
                    correlation_products(2 * i + u, u)
                for u in (0, 1):
                    pick_nine(2 * i + u, u)
                for u in (0, 1):
                    delay_products(2 * i + u, u)
                for u in (0, 1):
                    b = 2 * i + u
                    dve.wait_ge(inv_mm, b + 1)
                    v.scalar_tensor_tensor(X[:, b, :], bank[:, 4 * u, :], tg[:, 0:1], X[:, b, :],
                                           ALU.mult, ALU.add).then_inc(x_new[0][u], 1)
                    dve.wait_ge(x_new[0][u], i + 2)
                    token_stats(1, b, u)

            dve.wait_ge(scaled, 3)
            for c in range(C):
                dve.wait_ge(lora_mm, c + 1)
                v.tensor_tensor(W0[:, c, :], bank[:, c, :], W0[:, c, :], ALU.add).then_inc(lora_folded, 1)
            with dve.Fori(0, PAIRS) as i:
                for u in (0, 1):
                    normalise(1, 2 * i + u, u)
                for u in (0, 1):
                    b = 2 * i + u
                    dve.wait_ge(x_bias, b + 1)
                    dve.wait_ge(y_mm, b + 1)
                    v.tensor_tensor(X[:, b, :], bank[:, 4 * u + 1, :], big[:, u, 0, :], ALU.add).then_inc(x_new[1][u], 1)
                    dve.wait_ge(x_new[1][u], i + 2)
                    token_stats(2, b, u)

            for u in (0, 1):
                v.memset(vx[u][:, :, DH:VW], 1.0).then_inc(ready_bf, 1)

            def scores_less_max(b, k):
                s = bank[:, k % 4, :].rearrange("p (h s) -> p h s", h=4)
                dve.wait_ge(score_mm, QUADS * b + k + 1)
                v.reduce_max(mx[:, k % 4, :], s, AX).then_inc(row_max, 1)
                dve.wait_ge(row_max, QUADS * b + k + 1)
                if k >= 4:
                    dve.wait_ge(pT_mm, QUADS * b + k - 3)
                v.tensor_tensor(E[k % 4], s, mx[:, k % 4, :].unsqueeze(2).broadcast_to([P, 4, S]),
                                ALU.subtract).then_inc(less_max, 1)

            def attended(b, u, half):
                m = bank[:, 6 + half, 0:GROUPS * 2 * VW].rearrange("p (h w) -> p h w", w=VW)
                dve.wait_ge(av_mm, QUADS * b + 4 * half + 4)
                v.reciprocal(iden[:, half, :], m[:, :, DH]).then_inc(inv_den, 1)
                dve.wait_ge(inv_den, 2 * b + half + 1)
                o = att[u][:, half * 256:(half + 1) * 256].rearrange("p (h w) -> p h w", w=DH)
                v.tensor_tensor(o, m[:, :, 0:DH], iden[:, half, :].unsqueeze(2).broadcast_to([P, 2 * GROUPS, DH]),
                                ALU.mult).then_inc(att_set, 1)

            with dve.Fori(0, PAIRS) as i:
                for u in (0, 1):
                    b = 2 * i + u
                    normalise(2, b, u)
                    dve.wait_ge(cT_mm[u], i + 2)
                    v.tensor_copy(cT[:, u, :], bank[:, 5, :]).then_inc(cT_out, 1)
                    dve.wait_ge(kv_mm, b + 1)
                    for e in (0, 1):
                        v.tensor_scalar(kEO[u][:, e, :], bank[:, 1, 0:S], par[:, e:e + 1], None, ALU.mult).then_inc(kv_out, 1)
                    v.tensor_copy(vx[u][:, :, 0:DH], bank[:, 1, S:2 * S].rearrange("p (g w) -> p g w", w=DH)).then_inc(kv_out, 1)
                    for k in range(QUADS):
                        scores_less_max(b, k)
                        if k == 6:
                            attended(b, u, 0)
                    attended(b, u, 1)
                    dve.wait_ge(o_mm, b + 1)
                    v.tensor_tensor(X[:, b, :], bank[:, 5, :], X[:, b, :], ALU.add).then_inc(x_new[2][u], 1)
                    dve.wait_ge(x_new[2][u], i + 2)
                    token_stats(3, b, u)

            def choose_experts(b, u):
                s = bank[:, 4 * u + 1, 0:EXPERTS]
                dve.wait_ge(r_mm, b + 1)
                settle()
                v.max(rt[:, u, 0, :], s).then_inc(r_top, 1)
                dve.wait_ge(r_top, b + 1)
                v.tensor_scalar(rs[:, u, 0:1], rt[:, u, 0, 0:1], -1.0, None, ALU.mult).then_inc(r_neg, 1)
                v.match_replace(rl[:, u, 0, :], rt[:, u, 0, :], s, TAKEN).then_inc(r_less, 1)
                dve.wait_ge(r_less, b + 1)
                settle()
                v.max(rt[:, u, 1, :], rl[:, u, 0, :]).then_inc(r_top2, 1)
                dve.wait_ge(r_top2, b + 1)
                settle()
                v.match_replace(rl[:, u, 1, :], rt[:, u, 1, :], rl[:, u, 0, :], TAKEN).then_inc(r_less2, 1)
                dve.wait_ge(r_less2, b + 1)
                dve.wait_ge(r_exp, b + 1)
                v.scalar_tensor_tensor(rk[:, u, :], rl[:, u, 1, :], TAKEN, re[:, u, :],
                                       ALU.is_equal, ALU.mult).then_inc(r_kept, 1)
                dve.wait_ge(r_kept, b + 1)
                v.reduce_sum(rs[:, u, 1:2], rk[:, u, :], AX).then_inc(r_sum, 1)
                dve.wait_ge(r_sum, b + 1)
                v.reciprocal(rs[:, u, 2:3], rs[:, u, 1:2]).then_inc(r_inv, 1)
                dve.wait_ge(r_inv, b + 1)
                v.tensor_scalar(G[:, u, :], rk[:, u, :], rs[:, u, 2:3], None, ALU.mult).then_inc(gate_set, 1)
                dve.wait_ge(gate_set, b + 1)
                for q in (0, 1):
                    dve.wait_ge(h_mm, 2 * b + q + 1)
                    v.tensor_tensor(hg[u][:, 32 * q:32 * q + 32, :],
                                    bank[:, 4 * u + 2 + q, :].rearrange("p (k r) -> p k r", r=RANK),
                                    G[:, u, 32 * q:32 * q + 32].unsqueeze(2).broadcast_to([P, 32, RANK]),
                                    ALU.mult).then_inc(hg_set, 1)

            with dve.Fori(0, PAIRS) as i:
                for u in (0, 1):
                    normalise(3, 2 * i + u, u)
                for u in (0, 1):
                    choose_experts(2 * i + u, u)
                for u in (0, 1):
                    b = 2 * i + u
                    dve.wait_ge(e_mm, b + 1)
                    v.tensor_tensor(X[:, b, :], bank[:, 4 * u + 2, :], X[:, b, :], ALU.add).then_inc(x_new[3][u], 1)

        @block.tensor
        def _(pe):
            t = nc.tensor

            def mm(o, l, r, start=True, stop=True):
                return t.matmul(o, l, r, start=start, stop=stop)

            def transposes(o, src):
                for c in range(C):
                    last = t.transpose(o[:, c * P:(c + 1) * P], src[:, c * P:(c + 1) * P], ident)
                return last

            pe.wait_ge(mats_in, 16)

            with pe.Fori(0, PAIRS) as i:
                for u in (0, 1):
                    b, k = 2 * i + u, 4 * u
                    c_in = ctx_s[:, u, :]
                    pe.wait_ge(x_new[0][u], i + 1)
                    pe.wait_ge(ctx_ld[u], 16 * i + 16)
                    mm(bank[:, k + 0, :], mat["FB1"], c_in).then_inc(b1_mm, 1)
                    mm(bank[:, k + 1, :], mat["FB2"], c_in).then_inc(b2_mm, 1)
                    mm(bank[:, k + 3, :], mat["FC1"], c_in).then_inc(c1_mm, 1)
                    pe.wait_ge(normed[0], b + 1)
                    mm(bank[:, k + 2, :], mat["FA"], xn[:, u, :]).then_inc(a_mm, 1)
                    pe.wait_ge(b1_out, b + 1)
                    mm(bank[:, k + 0, :], mat["FC2"], c_in).then_inc(c2_mm[u], 1)
                for u in (0, 1):
                    b, k = 2 * i + u, 4 * u
                    pe.wait_ge(b2_out, b + 1)
                    pe.wait_ge(corr_prod, 2 * b + 2)
                    for c in range(C):
                        cs = slice(c * P, (c + 1) * P)
                        mm(bank[:, k + 1, cs], spec[u][0][:, cs], mat["G1"], stop=False)
                        last = mm(bank[:, k + 1, cs], spec[u][1][:, cs], mat["G2"], start=False)
                    last.then_inc(corr_mm, 1)
                for u in (0, 1):
                    b, k = 2 * i + u, 4 * u
                    pe.wait_ge(w_built, C * b + C)
                    for c in range(C):
                        last = t.transpose(bank[:, k + 2, c * P:(c + 1) * P], wts[:, u, c, :], ident)
                    last.then_inc(wt_mm, 1)
                    pe.wait_ge(c1_out, b + 1)
                    pe.wait_ge(wt_out, b + 1)
                    mm(bank[:, k + 3, :], mat["FA"], wT[:, u, :]).then_inc(we_mm, 1)
                    mm(bank[:, k + 1, :], mat["FO"], wT[:, u, :]).then_inc(wo_mm, 1)
                for u in (0, 1):
                    b, k = 2 * i + u, 4 * u
                    pe.wait_ge(c2_out, b + 1)
                    for n, name in enumerate(("H1", "H2", "J1", "J2")):
                        pe.wait_ge(spec_prod, 4 * b + n + 1)
                        last = mm(bank[:, k, :], mat[name], spec[u][n], start=n == 0, stop=n == 3)
                    last.then_inc(inv_mm, 1)

            pe.wait_ge(lora_in, 16 * 5)
            pe.wait_ge(scaled, 3)
            pe.wait_ge(x_new[0][0], PAIRS + 1)
            for c in range(C):
                mm(bank[:, c, :], LA[:, c * P:(c + 1) * P], LB[:]).then_inc(lora_mm, 1)
            pe.wait_ge(lora_folded, C)
            with pe.Fori(0, PAIRS) as i:
                for u in (0, 1):
                    b = 2 * i + u
                    pe.wait_ge(normed[1], b + 1)
                    transposes(bank[:, 4 * u, :], xn[:, u, :]).then_inc(xT_mm[1], 1)
                for u in (0, 1):
                    b = 2 * i + u
                    pe.wait_ge(x_new[1][u], i + 1)
                    pe.wait_ge(xT_out[1], b + 1)
                    for c in range(C):
                        last = mm(bank[:, 4 * u + 1, :], xT[:, u, c, :], W0[:, c, :], c == 0, c == C - 1)
                    last.then_inc(y_mm, 1)

            pe.wait_ge(attn_in, 16 * 4)
            pe.wait_ge(scaled, 5)
            pe.wait_ge(ready_bf, 4)

            def scores(b, u, half):
                for r in range(4):
                    if half == 0:
                        if r < 2:
                            pe.wait_ge(q_out if r == 0 else kv_out, b + 1 if r == 0 else 3 * b + 3)
                    else:
                        pe.wait_ge(less_max, QUADS * b + r + 1)
                    mm(bank[:, r, :], ident_bf[:], never[:].unsqueeze(1).broadcast_to([P, 4, S]), stop=False)
                for jl in (0, 1):
                    for r in range(4):
                        rows = slice(32 * r, 32 * r + 32)
                        j = 2 * half + jl
                        last = mm(bank[:, r, jl * 256:(jl + 1) * 256], qT[u][rows, j * P:(j + 1) * P],
                                  kEO[u][rows, :, :], start=False, stop=jl == 1)
                        if jl == 1:
                            last.then_inc(score_mm, 1)

            def turn_probs(b, k):
                if k >= 2:
                    pe.wait_ge(pT_out, QUADS * b + k - 1)
                pe.wait_ge(probs, QUADS * b + k + 1)
                for h in range(4):
                    last = t.transpose(bank[:, 4 + k % 2, h * P:(h + 1) * P], E[k % 4][:, h, :], ident)
                last.then_inc(pT_mm, 1)

            def attend(b, u, k):
                half, r = k // 4, k % 4
                pe.wait_ge(pT_out, QUADS * b + k + 1)
                for jl in (0, 1):
                    for e in (0, 1):
                        g = 2 * r + e
                        at = (g * 2 + jl) * VW
                        last = mm(bank[:, 6 + half, at:at + VW], ET[k % 2][:, 2 * jl + e, :], vx[u][:, g, :])
                last.then_inc(av_mm, 1)

            with pe.Fori(0, PAIRS) as i:
                for u in (0, 1):
                    b = 2 * i + u
                    pe.wait_ge(normed[2], b + 1)
                    transposes(bank[:, 4, :], xn[:, u, :]).then_inc(xT_mm[2], 1)
                    pe.wait_ge(ctx_ld[u], 16 * i + 16 * PAIRS + 16)
                    transposes(bank[:, 5, :], ctx_s[:, u, :]).then_inc(cT_mm[u], 1)
                    pe.wait_ge(xT_out[2], b + 1)
                    for j in range(4):
                        for c in range(C):
                            last = mm(bank[:, 0, j * P:(j + 1) * P], WQ[:, c, j * P:(j + 1) * P], xT[:, u, c, :],
                                      c == 0, c == C - 1)
                    last.then_inc(q_mm, 1)
                    pe.wait_ge(cT_out, b + 1)
                    for c in range(C):
                        mm(bank[:, 1, 0:P], WK[:, c, :], cT[:, u, c * P:(c + 1) * P], c == 0, c == C - 1)
                    for c in range(C):
                        last = mm(bank[:, 1, P:2 * P], cT[:, u, c * P:(c + 1) * P], WV[:, c, :], c == 0, c == C - 1)
                    last.then_inc(kv_mm, 1)
                    pe.wait_ge(kv_out, 3 * b + 3)
                    scores(b, u, 0)
                    for k in range(QUADS):
                        turn_probs(b, k)
                        if k == 3:
                            attend(b, u, 2)
                            scores(b, u, 1)
                        elif k > 0:
                            attend(b, u, k - 1)
                    attend(b, u, QUADS - 1)
                    pe.wait_ge(att_set, 2 * b + 2)
                    transposes(bank[:, 4, :], att[u]).then_inc(aT_mm, 1)
                    pe.wait_ge(aT_out, b + 1)
                    for c in range(C):
                        last = mm(bank[:, 5, :], attT[u][:, c, :], WO[:, c, :], c == 0, c == C - 1)
                    last.then_inc(o_mm, 1)

            pe.wait_ge(moe_in, 16 * 3)
            pe.wait_ge(scaled, 6)
            with pe.Fori(0, PAIRS) as i:
                for u in (0, 1):
                    b = 2 * i + u
                    pe.wait_ge(x_new[3][u], i + 1)
                    pe.wait_ge(normed[3], b + 1)
                    transposes(bank[:, 4 * u, :], xn[:, u, :]).then_inc(xT_mm[3], 1)
                for u in (0, 1):
                    b, k = 2 * i + u, 4 * u
                    pe.wait_ge(xT_out[3], b + 1)
                    for c in range(C):
                        last = mm(bank[:, k + 1, 0:EXPERTS], xT[:, u, c, :], WR[:, c, :], c == 0, c == C - 1)
                    last.then_inc(r_mm, 1)
                    for q in (0, 1):
                        for c in range(C):
                            last = mm(bank[:, k + 2 + q, :], xT[:, u, c, :], MA[:, c, q * D:(q + 1) * D], c == 0, c == C - 1)
                        last.then_inc(h_mm, 1)
                for u in (0, 1):
                    b, k = 2 * i + u, 4 * u
                    hf = hg[u].rearrange("p k r -> p (k r)")
                    for q in (0, 1):
                        pe.wait_ge(hg_set, 2 * b + q + 1)
                        transposes(bank[:, k + q, :], hf[:, q * D:(q + 1) * D]).then_inc(hT_mm, 1)
                for u in (0, 1):
                    b, k = 2 * i + u, 4 * u
                    for c in range(KC):
                        if c % C == 0:
                            pe.wait_ge(hT_out, 2 * b + c // C + 1)
                        last = mm(bank[:, k + 2, :], hT[u][:, c, :], MB[:, c, :], c == 0, c == KC - 1)
                    last.then_inc(e_mm, 1)


def kernel(x, ctx_4096, mask_SxS2_bk0, g_xattn, g_ffn, L0_ffn_lora_A, L0_ffn_lora_B, L0_ffn_W, L0_ffn_bias,
           L0_ffn_lora_weights, L1_xattn_w_q, L1_xattn_w_k, L1_xattn_w_v, L1_xattn_w_out, L1_ffn_A, L1_ffn_B,
           L1_ffn_Wr):
    import concourse.bacc as bacc
    from concourse.bass_utils import run_bass_kernel_spmd

    def rows_by_chunk(w):
        return w.reshape(-1, P, w.shape[-1]).transpose(1, 0, 2)

    asnp = np.asarray
    g_x, g_f = asnp(g_xattn), asnp(g_ffn)
    gates = np.broadcast_to(np.stack([g_x[0], g_f[0], g_x[1], g_f[1]]), (P, 4))
    wq = asnp(L1_xattn_w_q).reshape(GROUPS, HPG, DH, D).transpose(1, 0, 2, 3).reshape(D, D).T
    wo = asnp(L1_xattn_w_out).T.reshape(GROUPS, 2, 2, DH, D).transpose(1, 0, 2, 3, 4).reshape(D, D)
    m = transform_matrices()
    rows = np.arange(P) // DH % 2
    arrays = {
        "x": asnp(x), "ctx": asnp(ctx_4096), "mask": asnp(mask_SxS2_bk0), "gates": gates,
        "w_base": rows_by_chunk(asnp(L0_ffn_W).T),
        "lora_a": asnp(L0_ffn_lora_A).reshape(P, D),
        "lora_b": asnp(L0_ffn_lora_B).transpose(0, 2, 1).reshape(P, D),
        "lora_w": np.repeat(asnp(L0_ffn_lora_weights), P // 8).reshape(P, 1),
        "bias": np.broadcast_to(asnp(L0_ffn_bias), (P, D)),
        "wq": rows_by_chunk(wq), "wk": rows_by_chunk(asnp(L1_xattn_w_k).T), "wv": rows_by_chunk(asnp(L1_xattn_w_v).T),
        "wo": rows_by_chunk(wo),
        "moe_a": rows_by_chunk(asnp(L1_ffn_A).reshape(KR, D).T),
        "moe_b": rows_by_chunk(asnp(L1_ffn_B).transpose(0, 2, 1).reshape(KR, D)),
        "w_router": rows_by_chunk(asnp(L1_ffn_Wr).T),
        "mats": np.stack([m[n] for n in MATS], 1).astype(np.float32),
        "parity": np.stack([rows == 0, rows == 1], 1).astype(np.float32),
    }
    nc = bacc.Bacc("TRN2", target_bir_lowering=False, num_devices=1)
    ins, args = {}, []
    for name, a in arrays.items():
        a = np.ascontiguousarray(a)
        ins[f"in_{name}"] = a
        args.append(nc.dram_tensor(f"in_{name}", a.shape, mybir.dt.from_np(a.dtype), kind="ExternalInput").ap())
    out = nc.dram_tensor("out", (B, S, D), F32, kind="ExternalOutput").ap()
    flamingo_kernel(nc, *args, out)
    r = run_bass_kernel_spmd(nc, [ins], core_ids=[0])
    return r.results[0]["out"]
```

```python
from contextlib import ExitStack

import numpy as np

import concourse.bass as bass
from concourse import mybir

F32 = mybir.dt.float32
BF16 = mybir.dt.bfloat16
F32R = mybir.dt.float32r
ALU = mybir.AluOpType
ACT = mybir.ActivationFunctionType
AX = mybir.AxisListType.X

B, S, D = 8, 128, 512
P = 128
C = D // P
PAIRS = B // 2
EPS = 1e-5

DELAYS = 9
TAKEN = -2.0 ** 127
STAND_IN = -1.5 * 2.0 ** 127
FILL = 7

HEADS, GROUPS, DH = 32, 8, 16
HPG = HEADS // GROUPS
PAIRS_G = GROUPS // 2
VW = DH + 1
SLOTS = (0, 1, 0), (0, 0, 1)
TOP_ROW = 3 * 32
STACK = TOP_ROW + 4

EXPERTS, TOPK, RANK = 64, 16, 16
KR = EXPERTS * RANK
KC = KR // P

MATS = ["FA", "FB2", "FC1", "FC2", "FO", "G1", "G2", "H1", "H2", "J1", "J2", "ID"]


def transform_matrices():
    t = np.arange(S)
    r = np.arange(S)
    re = r <= S // 2
    k = np.where(re, r, r - S // 2)
    a = 2 * np.pi * np.outer(k, t) / S
    cos, sin = np.cos(a), np.sin(a)
    fa = np.where(re[:, None], cos, -sin)
    fb2 = -sin.copy()
    fb2[0, :] = t == S - 1
    w = np.where((k == 0) | (k == S // 2), 1.0, 2.0)[:, None] / S
    g1 = np.where(re[:, None], w * cos, -w * sin)
    g2 = np.where(re[:, None], w * sin, w * cos)
    h1 = 0.5 * np.where(re[:, None], w * cos, w * sin)
    h2 = 0.5 * np.where(re[:, None], -w * sin, w * cos)
    h2[0, :] = 0.5
    hr = r < S // 2
    kk = np.where(hr, r, r - S // 2) + 0.5
    o = 2 * np.pi * np.outer(kk, t) / S
    oc, os = np.cos(o), np.sin(o)
    less_last = np.eye(S)
    less_last[:, S - 1] -= 1.0
    fo = np.where(hr[:, None], oc, -os)
    j1 = (1.0 / S) * np.where(hr[:, None], oc, os)
    j2 = (1.0 / S) * np.where(hr[:, None], -os, oc)
    fb1 = cos
    mats = {"FA": fa.T, "FB1": fb1.T, "FB2": fb2.T, "FC1": (oc @ less_last).T, "FC2": (-os @ less_last).T,
            "FO": fo.T, "G1": g1, "G2": g2, "H1": h1, "H2": h2, "J1": j1, "J2": j2, "ID": np.eye(S)}
    return mats


MATS = list(transform_matrices())


def flamingo_kernel(nc, x, ctx_in, mask, mask_t, gates, w_base, lora_a, lora_b, lora_w, bias, wq, wk, wv, wo,
                    moe_a, moe_b, w_router, mats, parity, out):
    with ExitStack() as st:
        def sb(name, shape, dt=F32):
            return st.enter_context(nc.sbuf_tensor(name, shape, dt))

        def sem(name):
            return st.enter_context(nc.semaphore(name))

        def sems(name):
            return [sem(f"{name}{u}") for u in (0, 1)]

        X = sb("X", [P, B, D])
        stats = sb("stats", [P, B, 2])
        rstd = sb("rstd", [P, B])
        ident = sb("ident", [P, P])[:]
        ident_bf = sb("ident_bf", [P, P], BF16)
        mask_u8 = sb("mask_u8", [P, 2, S], mybir.dt.uint8)
        never = sb("never", [P, 2, S], BF16)
        par = sb("par", [P, 4])
        g_in = sb("g_in", [P, 4])
        tg = sb("tg", [P, 4])
        WQ = sb("WQ", [P, 2, C, D], F32R)
        WK = sb("WK", [P, 2, C, P], F32R)
        WV = sb("WV", [P, 2, C, P], F32R)
        WO = sb("WO", [P, 2, C, D], F32R)
        raw = sb("raw", [P, 4 * D])
        zero_eps = sb("zero_eps", [P, 2])
        neg_half = sb("neg_half", [P, 1])
        ctx_s = sb("ctx_s", [P, 2, D])
        xn = sb("xn", [P, 2, D])
        bn = sb("bn", [P, 2, 6])
        mv = sb("mv", [P, 2, 2])
        tick = sb("tick", [P, 1])
        xT = sb("xT", [P, 2, 2, C, P], F32R)

        early = ExitStack()

        def sb1(name, shape, dt=F32):
            return early.enter_context(nc.sbuf_tensor(name, shape, dt))

        M = sb1("M", [P, len(MATS), S])
        mat = {n: M[:, k, :] for k, n in enumerate(MATS)}
        W0 = sb1("W0", [P, C, D])
        W0p = sb1("W0p", [P, 2, C, D], F32R)
        LA = sb1("LA", [P, D])
        LB = sb1("LB", [P, D])
        lw = sb1("lw", [P, 2])
        BI = sb1("BI", [P, D])
        spectra = sb1("spectra", [P, 2, 4, D])
        products = sb1("products", [P, 2, 4, D])
        B1s, B2s, C1s, C2s = ([spectra[:, u, k, :] for u in (0, 1)] for k in range(4))
        spec = [[products[:, u, k, :] for k in range(4)] for u in (0, 1)]
        x_plus_bias = [spectra[:, u, 0, :] for u in (0, 1)]
        less = sb1("less", [P, 2, 2, C, S + FILL])
        expc = sb1("expc", [P, 2, C, S])
        kept = sb1("kept", [P, 2, C, S])
        wts = sb1("wts", [P, 2, C, S])
        wT = sb1("wT", [P, 2, D])
        top9 = sb1("top9", [P, 2, C, DELAYS])
        nxt = sb1("nxt", [P, 2, C, 8])
        ninth = sb1("ninth", [P, 2, C, 8])
        ntop = sb1("ntop", [P, 2, C])
        vals = sb1("vals", [P, 2, C, DELAYS])
        vsum = sb1("vsum", [P, 2, 2, C])
        early.close()

        MA = sb("MA", [P, 2, C, KR], F32R)
        MB = sb("MB", [P, 2, KC, D], F32R)
        WR = sb("WR", [P, 2, C, EXPERTS], F32R)
        cT = sb("cT", [P, C, 2, 2, P], F32R)
        qp = sb("qp", [P, 2, 2, HPG, S], F32R)
        kp = sb("kp", [P, 2, 2, 2, S], F32R)
        kf = sb("kf", [P, 2, 2, S])
        qst = sb("qst", [P, 2, PAIRS_G, D], F32R)
        kst = sb("kst", [P, 2, PAIRS_G, 2, S], F32R)
        vx = sb("vx", [P, 2, GROUPS, VW])
        xT3 = xT.rearrange("p u w c n -> p (u w c n)").rearrange("p (c w u n) -> p c w u n", c=C, w=2, u=2)
        att, aT = xn, xT
        ET = sb("ET", [P, 4, HPG, S])
        mx = sb("mx", [P, 2, 2, PAIRS_G, HPG])
        mT = sb("mT", [HEADS, 2, 2, S], F32R)
        iden = sb("iden", [P, 2, 4 * HPG])
        hg = [ET[:, 2 * u:2 * u + 2, :, :].rearrange("p a h (k r) -> p (a h k) r", r=RANK) for u in (0, 1)]
        hT = [qst[:, u, :, :].rearrange("p a (c n) -> p a c n", n=P).rearrange("p (w a) c n -> p w (a c) n", w=2) for u in (0, 1)]
        rl = ctx_s[:, :, 0:2 * EXPERTS].rearrange("p u (k e) -> p u k e", k=2)
        re, rk, G = (ctx_s[:, :, k * EXPERTS:(k + 1) * EXPERTS] for k in (2, 3, 4))
        rt = ctx_s[:, :, 5 * EXPERTS:5 * EXPERTS + 16].rearrange("p u (k e) -> p u k e", k=2)
        rs = ctx_s[:, :, 5 * EXPERTS + 16:5 * EXPERTS + 20]

        q_turn = nc.dram_tensor("q_turn", (P, 2, 2, HPG * S), F32, kind="Internal").ap()
        k_turn = nc.dram_tensor("k_turn", (P, 2, 2, 2 * S), F32, kind="Internal").ap()

        bank = st.enter_context(nc.psum_tensor("bank", [P, 8, D], F32))

        x_in, ctx_ld = [sem(f"x_in{b}") for b in range(B)], sems("ctx_ld")
        mats_in, gate_in, mask_in = sem("mats_in"), sem("gate_in"), sem("mask_in")
        lora_in = sem("lora_in")
        raw_in, raw_scaled, raw_high, raw_split = (sem(n) for n in ("raw_in", "raw_scaled", "raw_high", "raw_split"))
        consts_set, tanh_done, scaled = sem("consts_set"), sem("tanh_done"), sem("scaled")
        ready_bf = sem("ready_bf")
        bn_done = [sem(f"bn_done{p}") for p in range(4)]
        mv_done = [sem(f"mv_done{p}") for p in range(4)]
        stats_done = [sem(f"stats_done{p}") for p in range(4)]
        rstd_done = [sem(f"rstd_done{p}") for p in range(4)]
        normed = [sem(f"normed{p}") for p in range(4)]
        x_new = [sems(f"x_new{p}_") for p in range(4)]

        b1_mm, b2_mm, a_mm, c1_mm = (sem(n) for n in ("b1_mm", "b2_mm", "a_mm", "c1_mm"))
        c2_mm, cT_mm = sems("c2_mm"), sems("cT_mm")
        b1_out, b2_out, c1_out, c2_out = (sem(n) for n in ("b1_out", "b2_out", "c1_out", "c2_out"))
        corr_prod, corr_mm = sem("corr_prod"), sem("corr_mm")
        top8, neg_top, less8, next8, ninth_set = (sem(n) for n in ("top8", "neg_top", "less8", "next8", "ninth_set"))
        less9, kept_mask, vals_sub, vals_exp = (sem(n) for n in ("less9", "kept_mask", "vals_sub", "vals_exp"))
        exp_c, vals_sum, inv_sum, w_built = (sem(n) for n in ("exp_c", "vals_sum", "inv_sum", "w_built"))
        wt_mm, wt_out, we_mm, wo_mm, spec_prod, inv_mm = (sem(n) for n in ("wt_mm", "wt_out", "we_mm", "wo_mm", "spec_prod", "inv_mm"))

        lora_mm, lora_folded, w0_high, w0_low = (sem(n) for n in ("lora_mm", "lora_folded", "w0_high", "w0_low"))
        x_bias = sem("x_bias")
        xT_mm = [sem(f"xT_mm{p}") for p in range(4)]
        xT_high = [sem(f"xT_high{p}") for p in range(4)]
        xT_low = [sem(f"xT_low{p}") for p in range(4)]
        y_mm = sem("y_mm")

        cT_high, cT_low, q_mm, q_high, q_low, k_mm, v_mm, k_set, k_high, k_low, v_set = (
            sem(n) for n in ("cT_high", "cT_low", "q_mm", "q_high", "q_low", "k_mm", "v_mm", "k_set", "k_high", "k_low", "v_set"))
        ones_set = sem("ones_set")
        stacked, maxima_in = sems("stacked"), sems("maxima_in")
        q_away, k_away = sem("q_away"), sem("k_away")
        score_mm, row_max, mT_mm, mT_high, mT_low = (sem(n) for n in ("score_mm", "row_max", "mT_mm", "mT_high", "mT_low"))
        less_mm, probs, av_mm = (sem(n) for n in ("less_mm", "probs", "av_mm"))
        inv_den, att_set, aT_mm, aT_high, aT_low, o_mm = (
            sem(n) for n in ("inv_den", "att_set", "aT_mm", "aT_high", "aT_low", "o_mm"))

        r_mm, h_mm, r_top, r_less, r_top2, r_less2, r_neg, r_exp, r_kept, r_sum, r_inv, gate_set = (
            sem(n) for n in ("r_mm", "h_mm", "r_top", "r_less", "r_top2", "r_less2", "r_neg", "r_exp",
                             "r_kept", "r_sum", "r_inv", "gate_set"))
        hg_set, hT_mm, hT_high, hT_low, e_mm, stored = (
            sem(n) for n in ("hg_set", "hT_mm", "hT_high", "hT_low", "e_mm", "stored"))

        staged = [(wq[:, c0:c0 + 4, :], WQ[:, :, c0:c0 + 4, :], None, 1.0) for c0 in (0,)]
        staged += [(wk, WK, None, 1.0), (wv, WV, None, 1.0), (wo, WO, 2, 1.0)]
        N_ATTN = len(staged)
        staged += [(w_router, WR, None, 1.0)]
        staged += [(moe_a[:, c0:c0 + 2, :], MA[:, :, c0:c0 + 2, :], None, 1.0) for c0 in (0, 2)]
        staged += [(moe_b[:, c0:c0 + 4, :], MB[:, :, c0:c0 + 4, :], 3, 2.0) for c0 in (0, 4)]

        def raw_view(like):
            return raw[:, 0:like.shape[1] * like.shape[2]].rearrange("p (c n) -> p c n", c=like.shape[1])

        RING, LESS_RING, AV_BANK, SPARE = (0, 1, 2), (3, 4), (5, 6), 7
        STEPS = 2 * GROUPS
        AHEAD = {0: ("x", 0), 1: ("x", 1), 2: ("c", 0), 4: ("c", 1), 6: ("q", 0), 9: ("q", 1), 11: ("k", 0), 13: ("v", 1)}
        AHEAD_BANK = {("x", 0): 0, ("x", 1): 1, ("c", 0): 2, ("c", 1): 0, ("q", 0): 1, ("q", 1): 2, ("k", 0): 0, ("v", 1): 2}

        block = st.enter_context(nc.Block())

        @block.sync
        def _(sp):
            for u in (0, 1):
                for p in range(4):
                    sp.sem_inc(x_new[p][u], 1)
            sp.dma_start(M[:], mats).then_inc(mats_in, 16)
            for u in (0, 1):
                sp.dma_start(ctx_s[:, u, :], ctx_in[u]).then_inc(ctx_ld[u], 16)
            for b in range(B):
                sp.dma_start(X[:, b, :], x[b]).then_inc(x_in[b], 16)
            sp.dma_start(raw_view(staged[0][0]), staged[0][0]).then_inc(raw_in, 16)
            with sp.Fori(0, PAIRS - 1) as i:
                for u in (0, 1):
                    sp.wait_ge(c2_mm[u], i + 1)
                    sp.dma_start(ctx_s[:, u, :], ctx_in[2 * i + u + 2]).then_inc(ctx_ld[u], 16)
            for n in range(1, N_ATTN):
                sp.wait_ge(raw_split, n)
                sp.dma_start(raw_view(staged[n][0]), staged[n][0]).then_inc(raw_in, 16)
            for n in range(N_ATTN, len(staged)):
                sp.wait_ge(raw_split, n)
                sp.dma_start(raw_view(staged[n][0]), staged[n][0]).then_inc(raw_in, 16)
            for u in (0, 1):
                sp.wait_ge(c2_mm[u], PAIRS)
                sp.dma_start(ctx_s[:, u, :], ctx_in[u]).then_inc(ctx_ld[u], 16)

            def stack(pair, after_group):
                sp.wait_ge(q_low, 2 * pair + 2)
                sp.dma_start(q_turn, qp[:].rearrange("p w u j n -> p w u (j n)").bitcast(F32)).then_inc(q_away, 16)
                sp.wait_ge(k_low, pair + 1)
                sp.dma_start(k_turn, kp[:].rearrange("p w u e n -> p w u (e n)").bitcast(F32)).then_inc(k_away, 16)
                sp.wait_ge(q_away, 16 * pair + 16)
                for u in (0, 1):
                    if after_group:
                        after_group(u)
                    for slot, part in enumerate(SLOTS[0]):
                        sp.dma_start(qst[32 * slot:32 * slot + 32, u, :, :].bitcast(F32),
                                     q_turn.rearrange("(r p) w u n -> w u p r n", p=32)[part, u]).then_inc(stacked[u], 16)
                    if u == 0:
                        sp.wait_ge(k_away, 16 * pair + 16)
                    for slot, part in enumerate(SLOTS[1]):
                        sp.dma_start(kst[32 * slot:32 * slot + 32, u, :, :, :].rearrange("p r e n -> p r (e n)").bitcast(F32),
                                     k_turn.rearrange("(r p) w u n -> w u p r n", p=32)[part, u]).then_inc(stacked[u], 16)

            def maxima(i):
                for u in (0, 1):
                    sp.wait_ge(mT_low, 2 * i + u + 1)
                    for e in (0, 1):
                        for part in (0, 1):
                            row = TOP_ROW + 2 * e + part
                            sp.dma_start(qst[row:row + 1, u, :, :].rearrange("p r (j n) -> p (r j) n", j=HPG).bitcast(F32),
                                         mT[16 * e:16 * e + 16, u, part, :].bitcast(F32)).then_inc(maxima_in[u], 16)

            stack(0, None)
            with sp.Fori(0, PAIRS - 1) as i:
                for u in (0, 1):
                    sp.wait_ge(cT_mm[u], i + 1)
                    sp.dma_start(ctx_s[:, u, :], ctx_in[2 * i + u + 2]).then_inc(ctx_ld[u], 16)
                maxima(i)
                stack(i + 1, lambda u: sp.wait_ge(less_mm, STEPS * i + GROUPS * (u + 1)))
            maxima(PAIRS - 1)
            with sp.Fori(0, PAIRS) as i:
                for u in (0, 1):
                    sp.wait_ge(x_new[3][u], i + 2)
                    sp.dma_start(out[2 * i + u], X[:, 2 * i + u, :]).then_inc(stored, 16)
            sp.wait_ge(stored, 16 * B)

        @block.gpsimd
        def _(pool):
            g = nc.gpsimd
            g.memset(zero_eps[:, 0:1], 0.0).then_inc(consts_set, 1)
            g.memset(zero_eps[:, 1:2], EPS).then_inc(consts_set, 1)
            g.memset(neg_half[:], -0.5).then_inc(consts_set, 1)
            g.memset(less[:], STAND_IN).then_inc(consts_set, 1)
            g.memset(ninth[:], STAND_IN).then_inc(consts_set, 1)
            pool.wait_ge(consts_set, 5)

            def inverse_std(p, b, u):
                pool.wait_ge(stats_done[p], b + 1)
                pool.wait_ge(consts_set, 5)
                g.tensor_tensor(rstd[:, bass.ds(b, 1)], stats[:, b, 1:2], neg_half[:], ALU.pow).then_inc(rstd_done[p], 1)

            for b in range(B):
                pool.wait_ge(stats_done[0], b + 1)
                g.tensor_tensor(rstd[:, b:b + 1], stats[:, b, 1:2], neg_half[:], ALU.pow).then_inc(rstd_done[0], 1)

            def split(n):
                src, parts, gate, factor = staged[n]
                w = raw_view(src)
                scales = sum(x[2] is not None for x in staged[:n])
                pool.wait_ge(raw_in, 16 * (n + 1))
                if gate is not None:
                    g.tensor_scalar(w, w, tg[:, gate:gate + 1], factor, ALU.mult, ALU.mult).then_inc(raw_scaled, 1)
                    pool.wait_ge(raw_scaled, scales + 1)
                g.tensor_copy(parts[:, 0], w).then_inc(raw_high, 1)
                pool.wait_ge(raw_high, n + 1)
                g.tensor_tensor(parts[:, 1], w, parts[:, 0].bitcast(F32), ALU.subtract).then_inc(raw_split, 1)

            pool.wait_ge(tanh_done, 1)
            pool.wait_ge(lora_in, 16 * 5)
            g.tensor_scalar(lw[:, 1:2], lw[:, 0:1], tg[:, 1:2], 2.0, ALU.mult, ALU.mult).then_inc(scaled, 1)
            pool.wait_ge(scaled, 1)
            g.tensor_scalar(LB[:], LB[:], lw[:, 1:2], 1.0, ALU.mult, ALU.mult).then_inc(scaled, 1)
            g.tensor_scalar(W0[:], W0[:], tg[:, 1:2], 1.0, ALU.mult, ALU.mult).then_inc(scaled, 1)
            g.tensor_scalar(BI[:], BI[:], tg[:, 1:2], 1.0, ALU.mult, ALU.mult).then_inc(scaled, 1)
            for n in range(N_ATTN):
                split(n)

            with pool.Fori(0, PAIRS) as i:
                for u in (0, 1):
                    inverse_std(1, 2 * i + u, u)
            pool.wait_ge(scaled, 4)
            pool.wait_ge(x_new[0][0], PAIRS + 1)
            pool.wait_ge(x_new[0][1], PAIRS + 1)
            with pool.Fori(0, PAIRS) as i:
                for u in (0, 1):
                    pool.wait_ge(x_new[1][u], i + 1)
                    pool.wait_ge(consts_set, 5)
                    g.tensor_tensor(x_plus_bias[u], X[:, 2 * i + u, :], BI[:], ALU.add).then_inc(x_bias, 1)
                for u in (0, 1):
                    inverse_std(2, 2 * i + u, u)
            for u in (0, 1):
                pool.wait_ge(x_new[1][u], PAIRS + 1)
            for n in range(N_ATTN, len(staged)):
                split(n)
            with pool.Fori(0, PAIRS) as i:
                for u in (0, 1):
                    inverse_std(3, 2 * i + u, u)

        @block.scalar
        def _(act):
            a = nc.scalar
            act.dma_start(g_in[:], gates).then_inc(gate_in, 16)
            act.dma_start(ident, mats[:, MATS.index("ID"), :]).then_inc(mats_in, 16)
            act.dma_start(mask_u8[:, 0, :], mask).then_inc(mask_in, 16)
            act.dma_start(mask_u8[:, 1, :], mask_t).then_inc(mask_in, 16)
            act.dma_start(par[:], parity).then_inc(mask_in, 16)
            act.dma_start(W0[:], w_base).then_inc(lora_in, 16)
            act.dma_start(LA[:], lora_a).then_inc(lora_in, 16)
            act.dma_start(LB[:], lora_b).then_inc(lora_in, 16)
            act.dma_start(lw[:, 0:1], lora_w).then_inc(lora_in, 16)
            act.dma_start(BI[:], bias).then_inc(lora_in, 16)
            act.wait_ge(gate_in, 16)
            a.activation(tg[:], g_in[:], ACT.Tanh).then_inc(tanh_done, 1)

            def copy(dst, src):
                return a.activation(dst, src, ACT.Copy)

            with act.Fori(0, PAIRS) as i:
                for u in (0, 1):
                    b, k = 2 * i + u, 4 * u
                    act.wait_ge(b1_mm, b + 1)
                    copy(B1s[u], bank[:, k + 0, :]).then_inc(b1_out, 1)
                    act.wait_ge(b2_mm, b + 1)
                    copy(B2s[u], bank[:, k + 1, :]).then_inc(b2_out, 1)
                    act.wait_ge(c1_mm, b + 1)
                    copy(C1s[u], bank[:, k + 3, :]).then_inc(c1_out, 1)
                    act.wait_ge(c2_mm[u], i + 1)
                    copy(C2s[u], bank[:, k + 0, :]).then_inc(c2_out, 1)
                for u in (0, 1):
                    b, k = 2 * i + u, 4 * u
                    act.wait_ge(neg_top, b + 1)
                    act.wait_ge(less8, C * b + C)
                    for c in range(C):
                        a.activation(expc[:, u, c, :], bank[:, k + 1, c * S:(c + 1) * S], ACT.Exp,
                                     bias=ntop[:, u, c:c + 1]).then_inc(exp_c, 1)
                    act.wait_ge(vals_sub, b + 1)
                    a.activation(vals[:, u, :, :], vals[:, u, :, :], ACT.Exp).then_inc(vals_exp, 1)
                for u in (0, 1):
                    b, k = 2 * i + u, 4 * u
                    act.wait_ge(wt_mm, b + 1)
                    copy(wT[:, u, :], bank[:, k + 2, :]).then_inc(wt_out, 1)

            for c in range(C):
                act.wait_ge(lora_folded, c + 1)
                copy(W0p[:, 0, c, :], W0[:, c, :]).then_inc(w0_high, 1)
            with act.Fori(0, PAIRS) as i:
                for u in (0, 1):
                    act.wait_ge(xT_mm[1], 2 * i + u + 1)
                    copy(xT[:, u, 0, :, :], bank[:, 4 * u, :]).then_inc(xT_high[1], 1)

            def ahead_high(pair, item, n):
                o = bank[:, AHEAD_BANK[item, n], :]
                if item == "x":
                    act.wait_ge(xT_mm[2], 2 * pair + n + 1)
                    copy(xT3[:, :, 0, n, :], o.rearrange("p (c n) -> p c n", c=C)).then_inc(xT_high[2], 1)
                elif item == "c":
                    act.wait_ge(cT_mm[n], pair + 1)
                    copy(cT[:, :, 0, n, :], o.rearrange("p (c n) -> p c n", c=C)).then_inc(cT_high, 1)
                elif item == "q":
                    act.wait_ge(q_mm, 2 * pair + n + 1)
                    for u in (0, 1):
                        copy(qp[:, 0, u, 2 * n:2 * n + 2, :],
                             o.rearrange("p (j u n) -> p j u n", j=2, u=2)[:, :, u, :]).then_inc(q_high, 1)
                elif item == "k":
                    act.wait_ge(k_set, 2 * pair + 2)
                    copy(kp[:, 0, :, :, :], kf[:]).then_inc(k_high, 1)

            def minus_maxima(i):
                for u in (0, 1):
                    act.wait_ge(mT_mm, 2 * i + u + 1)
                    a.activation(mT[:, u, 0, :], bank[0:HEADS, SPARE, 0:S], ACT.Copy, scale=-1.0).then_inc(mT_high, 1)

            def attention(i, ahead):
                minus_maxima(i)
                for s in range(STEPS):
                    if s >= 4:
                        act.wait_ge(av_mm, STEPS * i + s - 3)
                    act.wait_ge(less_mm, STEPS * i + s + 1)
                    a.activation(ET[:, s % 4, :, :], bank[:, LESS_RING[s % 2], :], ACT.Exp,
                                 scale=DH ** -0.5).then_inc(probs, 1)
                    if ahead and s in AHEAD:
                        ahead_high(i + 1, *AHEAD[s])
                    if s == 12:
                        act.wait_ge(aT_mm, 2 * i + 1)
                        copy(aT[:, 0, 0, :, :], bank[:, SPARE, :]).then_inc(aT_high, 1)
                act.wait_ge(aT_mm, 2 * i + 2)
                copy(aT[:, 1, 0, :, :], bank[:, SPARE, :]).then_inc(aT_high, 1)

            for item in AHEAD.values():
                ahead_high(0, *item)
            with act.Fori(0, PAIRS - 1) as i:
                attention(i, True)
            attention(PAIRS - 1, False)

            with act.Fori(0, PAIRS) as i:
                for u in (0, 1):
                    b = 2 * i + u
                    act.wait_ge(xT_mm[3], b + 1)
                    copy(xT[:, u, 0, :, :], bank[:, 4 * u, :]).then_inc(xT_high[3], 1)
                for u in (0, 1):
                    b = 2 * i + u
                    act.wait_ge(r_neg, b + 1)
                    act.wait_ge(r_less, b + 1)
                    a.activation(re[:, u, :], bank[:, 4 * u + 1, 0:EXPERTS], ACT.Exp, bias=rs[:, u, 0:1]).then_inc(r_exp, 1)
                for u in (0, 1):
                    for v in (0, 1):
                        act.wait_ge(hT_mm, 4 * i + 2 * u + v + 1)
                        copy(hT[u][:, 0, 4 * v:4 * v + 4, :], bank[:, 4 * u + v, :]).then_inc(hT_high, 1)

        @block.vector
        def _(dve):
            v = nc.vector

            def settle():
                v.memset(tick[:], 0.0)

            def token_stats(p, b, u):
                settle()
                v.bn_stats(bn[:, u, :], X[:, b, :]).then_inc(bn_done[p], 1)
                dve.wait_ge(bn_done[p], b + 1)
                settle()
                v.bn_aggr(mv[:, u, :], bn[:, u, :]).then_inc(mv_done[p], 1)
                dve.wait_ge(mv_done[p], b + 1)
                v.tensor_tensor(stats[:, b, :], mv[:, u, :], zero_eps[:], ALU.add).then_inc(stats_done[p], 1)

            def low(dst, whole, high):
                return v.tensor_tensor(dst, whole, high.bitcast(F32), ALU.subtract)

            def normalise(p, b, u):
                dve.wait_ge(rstd_done[p], b + 1)
                v.tensor_scalar(xn[:, u, :], X[:, b, :], stats[:, b, 0:1], rstd[:, bass.ds(b, 1)],
                                ALU.subtract, ALU.mult).then_inc(normed[p], 1)

            dve.wait_ge(consts_set, 5)
            for b in range(B):
                dve.wait_ge(x_in[b], 16)
                v.bn_stats(bn[:, b % 2, :], X[:, b, :]).then_inc(bn_done[0], 1)
                dve.wait_ge(bn_done[0], b + 1)
                v.bn_aggr(mv[:, b % 2, :], bn[:, b % 2, :]).then_inc(mv_done[0], 1)
                dve.wait_ge(mv_done[0], b + 1)
                v.tensor_tensor(stats[:, b, :], mv[:, b % 2, :], zero_eps[:], ALU.add).then_inc(stats_done[0], 1)
            dve.wait_ge(mats_in, 32)
            v.tensor_copy(ident_bf[:], ident).then_inc(ready_bf, 1)
            dve.wait_ge(mask_in, 48)
            v.tensor_scalar(never[:], mask_u8[:], 0.0, TAKEN, ALU.is_equal, ALU.mult).then_inc(ready_bf, 1)

            def correlation_products(b, u):
                k = 4 * u
                dve.wait_ge(a_mm, b + 1)
                dve.wait_ge(b1_out, b + 1)
                v.tensor_tensor(spec[u][0], bank[:, k + 2, :], B1s[u], ALU.mult).then_inc(corr_prod, 1)
                dve.wait_ge(b2_out, b + 1)
                v.tensor_tensor(spec[u][1], bank[:, k + 2, :], B2s[u], ALU.mult).then_inc(corr_prod, 1)

            def pick_nine(b, u):
                corr = bank[:, 4 * u + 1, :].rearrange("p (c s) -> p c s", c=C)
                dve.wait_ge(corr_mm, b + 1)
                settle()
                for c in range(C):
                    v.max(top9[:, u, c, 0:8], corr[:, c, :]).then_inc(top8, 1)
                dve.wait_ge(top8, C * b + C)
                v.tensor_scalar(ntop[:, u, :], top9[:, u, :, 0], -1.0, None, ALU.mult).then_inc(neg_top, 1)
                for c in range(C):
                    v.match_replace(less[:, u, 0, c, 0:S], top9[:, u, c, 0:8], corr[:, c, :], TAKEN).then_inc(less8, 1)
                dve.wait_ge(less8, C * b + C)
                settle()
                for c in range(C):
                    v.max(nxt[:, u, c, :], less[:, u, 0, c, 0:S]).then_inc(next8, 1)
                dve.wait_ge(next8, C * b + C)
                v.tensor_copy(ninth[:, u, :, 0], nxt[:, u, :, 0]).then_inc(ninth_set, 1)
                v.tensor_copy(top9[:, u, :, 8], nxt[:, u, :, 0]).then_inc(ninth_set, 1)
                dve.wait_ge(ninth_set, 2 * b + 2)
                v.tensor_tensor(vals[:, u, :, :], top9[:, u, :, :],
                                ntop[:, u, :].unsqueeze(2).broadcast_to([P, C, DELAYS]), ALU.add).then_inc(vals_sub, 1)
                for c in range(C):
                    v.match_replace(less[:, u, 1, c, :], ninth[:, u, c, :], less[:, u, 0, c, :], TAKEN).then_inc(less9, 1)
                dve.wait_ge(less9, C * b + C)
                v.tensor_scalar(kept[:, u, :, :], less[:, u, 1, :, 0:S], TAKEN, None, ALU.is_equal).then_inc(kept_mask, 1)
                dve.wait_ge(vals_exp, b + 1)
                v.reduce_sum(vsum[:, u, 0, :], vals[:, u, :, :], AX).then_inc(vals_sum, 1)
                dve.wait_ge(vals_sum, b + 1)
                v.reciprocal(vsum[:, u, 1, :], vsum[:, u, 0, :]).then_inc(inv_sum, 1)
                dve.wait_ge(inv_sum, b + 1)
                dve.wait_ge(kept_mask, b + 1)
                dve.wait_ge(exp_c, C * b + C)
                for c in range(C):
                    v.scalar_tensor_tensor(wts[:, u, c, :], expc[:, u, c, :], vsum[:, u, 1, c:c + 1],
                                           kept[:, u, c, :], ALU.mult, ALU.mult).then_inc(w_built, 1)

            def delay_products(b, u):
                k = 4 * u
                dve.wait_ge(we_mm, b + 1)
                v.tensor_tensor(spec[u][0], bank[:, k + 3, :], B1s[u], ALU.mult).then_inc(spec_prod, 1)
                v.tensor_tensor(spec[u][1], bank[:, k + 3, :], B2s[u], ALU.mult).then_inc(spec_prod, 1)
                dve.wait_ge(wo_mm, b + 1)
                v.tensor_tensor(spec[u][2], bank[:, k + 1, :], C1s[u], ALU.mult).then_inc(spec_prod, 1)
                v.tensor_tensor(spec[u][3], bank[:, k + 1, :], C2s[u], ALU.mult).then_inc(spec_prod, 1)

            with dve.Fori(0, PAIRS) as i:
                for u in (0, 1):
                    normalise(0, 2 * i + u, u)
                for u in (0, 1):
                    correlation_products(2 * i + u, u)
                for u in (0, 1):
                    pick_nine(2 * i + u, u)
                for u in (0, 1):
                    delay_products(2 * i + u, u)
                for u in (0, 1):
                    b = 2 * i + u
                    dve.wait_ge(inv_mm, b + 1)
                    v.scalar_tensor_tensor(X[:, b, :], bank[:, 4 * u, :], tg[:, 0:1], X[:, b, :],
                                           ALU.mult, ALU.add).then_inc(x_new[0][u], 1)
                    dve.wait_ge(x_new[0][u], i + 2)
                    token_stats(1, b, u)

            dve.wait_ge(scaled, 3)
            for c in range(C):
                dve.wait_ge(lora_mm, c + 1)
                v.tensor_tensor(W0[:, c, :], bank[:, c, :], W0[:, c, :], ALU.add).then_inc(lora_folded, 1)
            for c in range(C):
                dve.wait_ge(w0_high, c + 1)
                low(W0p[:, 1, c, :], W0[:, c, :], W0p[:, 0, c, :]).then_inc(w0_low, 1)
            with dve.Fori(0, PAIRS) as i:
                for u in (0, 1):
                    normalise(1, 2 * i + u, u)
                for u in (0, 1):
                    dve.wait_ge(xT_high[1], 2 * i + u + 1)
                    low(xT[:, u, 1, :, :], bank[:, 4 * u, :], xT[:, u, 0, :, :]).then_inc(xT_low[1], 1)
                for u in (0, 1):
                    b = 2 * i + u
                    dve.wait_ge(x_bias, b + 1)
                    dve.wait_ge(y_mm, b + 1)
                    v.tensor_tensor(X[:, b, :], bank[:, 4 * u + 1, :], x_plus_bias[u], ALU.add).then_inc(x_new[1][u], 1)
                    dve.wait_ge(x_new[1][u], i + 2)
                    token_stats(2, b, u)

            for u in (0, 1):
                v.memset(vx[:, u, :, DH:VW], 1.0).then_inc(ones_set, 1)
                for e in (0, 1):
                    rows = slice(TOP_ROW, STACK)
                    v.tensor_copy(kst[rows, u, :, e, :],
                                  par[rows, 2 + e:3 + e].unsqueeze(2).broadcast_to([4, PAIRS_G, S])).then_inc(ones_set, 1)

            def attended(b, u, half):
                m = bank[:, AV_BANK[half], 0:4 * HPG * VW].rearrange("p (h w) -> p h w", w=VW)
                dve.wait_ge(av_mm, GROUPS * b + 4 * half + 4)
                v.reciprocal(iden[:, half, :], m[:, :, DH]).then_inc(inv_den, 1)
                dve.wait_ge(inv_den, 2 * b + half + 1)
                o = att[:, u, half * 256:(half + 1) * 256].rearrange("p (h w) -> p h w", w=DH)
                v.tensor_tensor(o, m[:, :, 0:DH], iden[:, half, :].unsqueeze(2).broadcast_to([P, 4 * HPG, DH]),
                                ALU.mult).then_inc(att_set, 1)

            def attention_low(i, u):
                dve.wait_ge(aT_high, 2 * i + u + 1)
                low(aT[:, u, 1, :, :], bank[:, SPARE, :], aT[:, u, 0, :, :]).then_inc(aT_low, 1)

            def add_attention(i, u):
                b = 2 * i + u
                dve.wait_ge(o_mm, b + 1)
                v.tensor_tensor(X[:, b, :], bank[:, SPARE, :], X[:, b, :], ALU.add).then_inc(x_new[2][u], 1)
                dve.wait_ge(x_new[2][u], i + 2)
                token_stats(3, b, u)

            def ahead_low(pair, item, n):
                o = bank[:, AHEAD_BANK[item, n], :]
                if item == "x":
                    dve.wait_ge(xT_high[2], 2 * pair + n + 1)
                    low(xT3[:, :, 1, n, :], o.rearrange("p (c n) -> p c n", c=C), xT3[:, :, 0, n, :]).then_inc(xT_low[2], 1)
                elif item == "c":
                    dve.wait_ge(cT_high, 2 * pair + n + 1)
                    low(cT[:, :, 1, n, :], o.rearrange("p (c n) -> p c n", c=C), cT[:, :, 0, n, :]).then_inc(cT_low, 1)
                elif item == "q":
                    dve.wait_ge(q_high, 4 * pair + 2 * n + 2)
                    js = slice(2 * n, 2 * n + 2)
                    for u in (0, 1):
                        last = low(qp[:, 1, u, js, :], o.rearrange("p (j u n) -> p j u n", j=2, u=2)[:, :, u, :],
                                   qp[:, 0, u, js, :])
                    last.then_inc(q_low, 1)
                elif item == "k":
                    dve.wait_ge(k_mm, pair + 1)
                    for e in (0, 1):
                        v.tensor_scalar(kf[:, :, e, :], o[:, 0:2 * S].rearrange("p (u n) -> p u n", u=2), par[:, e:e + 1], None,
                                        ALU.mult).then_inc(k_set, 1)
                    values(pair, 0)
                    dve.wait_ge(k_high, pair + 1)
                    low(kp[:, 1, :, :, :], kf[:], kp[:, 0, :, :, :]).then_inc(k_low, 1)

            def values(pair, u):
                dve.wait_ge(v_mm, 2 * pair + u + 1)
                v.tensor_copy(vx[:, u, :, 0:DH], bank[:, AHEAD_BANK["kv"[u], u], (2 + u) * S:(3 + u) * S]
                              .rearrange("p (g w) -> p g w", w=DH)).then_inc(v_set, 1)

            def row_maxima(b, u):
                for n in range(8):
                    half, r = n // 4, n % 4
                    dve.wait_ge(score_mm, 8 * b + n + 1)
                    v.reduce_max(mx[:, u, :, r, 2 * half:2 * half + 2].rearrange("p e j -> p j e"),
                                 bank[:, RING[n % 3], :].rearrange("p (j e s) -> p j e s", j=2, e=2), AX).then_inc(row_max, 1)

            def maxima_low(b, u):
                dve.wait_ge(mT_high, b + 1)
                v.scalar_tensor_tensor(mT[:, u, 1, :], bank[0:HEADS, SPARE, 0:S], -1.0, mT[:, u, 0, :].bitcast(F32),
                                       ALU.mult, ALU.subtract).then_inc(mT_low, 1)

            def attention(i, ahead):
                row_maxima(2 * i, 0)
                maxima_low(2 * i, 0)
                if ahead:
                    for u in (0, 1):
                        normalise(2, 2 * i + 2 + u, u)
                row_maxima(2 * i + 1, 1)
                maxima_low(2 * i + 1, 1)
                for s in range(STEPS):
                    if ahead and s in AHEAD:
                        ahead_low(i + 1, *AHEAD[s])
                    if s in (5, 9, 13):
                        attended(2 * i + s // 13, s // 13, (s - 5) // 4 % 2)
                    if s == 12:
                        attention_low(i, 0)
                    if s == 15:
                        add_attention(i, 0)
                attended(2 * i + 1, 1, 1)
                if ahead:
                    values(i + 1, 1)
                attention_low(i, 1)
                add_attention(i, 1)

            for u in (0, 1):
                normalise(2, u, u)
            for item in AHEAD.values():
                ahead_low(0, *item)
            values(0, 1)
            with dve.Fori(0, PAIRS - 1) as i:
                attention(i, True)
            attention(PAIRS - 1, False)

            def choose_experts(b, u):
                s = bank[:, 4 * u + 1, 0:EXPERTS]
                dve.wait_ge(r_mm, b + 1)
                settle()
                v.max(rt[:, u, 0, :], s).then_inc(r_top, 1)
                dve.wait_ge(r_top, b + 1)
                v.tensor_scalar(rs[:, u, 0:1], rt[:, u, 0, 0:1], -1.0, None, ALU.mult).then_inc(r_neg, 1)
                v.match_replace(rl[:, u, 0, :], rt[:, u, 0, :], s, TAKEN).then_inc(r_less, 1)
                dve.wait_ge(r_less, b + 1)
                settle()
                v.max(rt[:, u, 1, :], rl[:, u, 0, :]).then_inc(r_top2, 1)
                dve.wait_ge(r_top2, b + 1)
                settle()
                v.match_replace(rl[:, u, 1, :], rt[:, u, 1, :], rl[:, u, 0, :], TAKEN).then_inc(r_less2, 1)
                dve.wait_ge(r_less2, b + 1)
                dve.wait_ge(r_exp, b + 1)
                v.scalar_tensor_tensor(rk[:, u, :], rl[:, u, 1, :], TAKEN, re[:, u, :],
                                       ALU.is_equal, ALU.mult).then_inc(r_kept, 1)
                dve.wait_ge(r_kept, b + 1)
                v.reduce_sum(rs[:, u, 1:2], rk[:, u, :], AX).then_inc(r_sum, 1)
                dve.wait_ge(r_sum, b + 1)
                v.reciprocal(rs[:, u, 2:3], rs[:, u, 1:2]).then_inc(r_inv, 1)
                dve.wait_ge(r_inv, b + 1)
                v.tensor_scalar(G[:, u, :], rk[:, u, :], rs[:, u, 2:3], None, ALU.mult).then_inc(gate_set, 1)
                dve.wait_ge(gate_set, b + 1)
                for q in (0, 1):
                    dve.wait_ge(h_mm, 2 * b + q + 1)
                    v.tensor_tensor(hg[u][:, 32 * q:32 * q + 32, :],
                                    bank[:, 4 * u + 2 + q, :].rearrange("p (k r) -> p k r", r=RANK),
                                    G[:, u, 32 * q:32 * q + 32].unsqueeze(2).broadcast_to([P, 32, RANK]),
                                    ALU.mult).then_inc(hg_set, 1)

            with dve.Fori(0, PAIRS) as i:
                for u in (0, 1):
                    normalise(3, 2 * i + u, u)
                for u in (0, 1):
                    dve.wait_ge(xT_high[3], 2 * i + u + 1)
                    low(xT[:, u, 1, :, :], bank[:, 4 * u, :], xT[:, u, 0, :, :]).then_inc(xT_low[3], 1)
                for u in (0, 1):
                    choose_experts(2 * i + u, u)
                for u in (0, 1):
                    for q in (0, 1):
                        dve.wait_ge(hT_high, 4 * i + 2 * u + q + 1)
                        low(hT[u][:, 1, 4 * q:4 * q + 4, :], bank[:, 4 * u + q, :], hT[u][:, 0, 4 * q:4 * q + 4, :]).then_inc(hT_low, 1)
                for u in (0, 1):
                    b = 2 * i + u
                    dve.wait_ge(e_mm, b + 1)
                    v.tensor_tensor(X[:, b, :], bank[:, 4 * u + 2, :], X[:, b, :], ALU.add).then_inc(x_new[3][u], 1)

        @block.tensor
        def _(pe):
            t = nc.tensor

            def mm(o, l, r, start=True, stop=True):
                return t.matmul(o, l, r, start=start, stop=stop)

            def mm3(o, l, r, start=True, stop=True):
                mm(o, l[0], r[0], start, False)
                mm(o, l[0], r[1], False, False)
                return mm(o, l[1], r[0], False, stop)

            def transposes(o, src):
                for c in range(C):
                    last = t.transpose(o[:, c * P:(c + 1) * P], src[:, c * P:(c + 1) * P], ident)
                return last

            pe.wait_ge(mats_in, 32)

            with pe.Fori(0, PAIRS) as i:
                for u in (0, 1):
                    b, k = 2 * i + u, 4 * u
                    c_in = ctx_s[:, u, :]
                    pe.wait_ge(x_new[0][u], i + 1)
                    pe.wait_ge(ctx_ld[u], 16 * i + 16)
                    mm(bank[:, k + 0, :], mat["FB1"], c_in).then_inc(b1_mm, 1)
                    mm(bank[:, k + 1, :], mat["FB2"], c_in).then_inc(b2_mm, 1)
                    mm(bank[:, k + 3, :], mat["FC1"], c_in).then_inc(c1_mm, 1)
                    pe.wait_ge(normed[0], b + 1)
                    mm(bank[:, k + 2, :], mat["FA"], xn[:, u, :]).then_inc(a_mm, 1)
                    pe.wait_ge(b1_out, b + 1)
                    mm(bank[:, k + 0, :], mat["FC2"], c_in).then_inc(c2_mm[u], 1)
                for u in (0, 1):
                    b, k = 2 * i + u, 4 * u
                    pe.wait_ge(b2_out, b + 1)
                    pe.wait_ge(corr_prod, 2 * b + 2)
                    for c in range(C):
                        cs = slice(c * P, (c + 1) * P)
                        mm(bank[:, k + 1, cs], spec[u][0][:, cs], mat["G1"], stop=False)
                        last = mm(bank[:, k + 1, cs], spec[u][1][:, cs], mat["G2"], start=False)
                    last.then_inc(corr_mm, 1)
                for u in (0, 1):
                    b, k = 2 * i + u, 4 * u
                    pe.wait_ge(w_built, C * b + C)
                    for c in range(C):
                        last = t.transpose(bank[:, k + 2, c * P:(c + 1) * P], wts[:, u, c, :], ident)
                    last.then_inc(wt_mm, 1)
                    pe.wait_ge(c1_out, b + 1)
                    pe.wait_ge(wt_out, b + 1)
                    mm(bank[:, k + 3, :], mat["FA"], wT[:, u, :]).then_inc(we_mm, 1)
                    mm(bank[:, k + 1, :], mat["FO"], wT[:, u, :]).then_inc(wo_mm, 1)
                for u in (0, 1):
                    b, k = 2 * i + u, 4 * u
                    pe.wait_ge(c2_out, b + 1)
                    for n, name in enumerate(("H1", "H2", "J1", "J2")):
                        pe.wait_ge(spec_prod, 4 * b + n + 1)
                        last = mm(bank[:, k, :], mat[name], spec[u][n], start=n == 0, stop=n == 3)
                    last.then_inc(inv_mm, 1)

            pe.wait_ge(lora_in, 16 * 5)
            pe.wait_ge(scaled, 3)
            pe.wait_ge(x_new[0][0], PAIRS + 1)
            for c in range(C):
                mm(bank[:, c, :], LA[:, c * P:(c + 1) * P], LB[:]).then_inc(lora_mm, 1)
            pe.wait_ge(w0_low, C)
            with pe.Fori(0, PAIRS) as i:
                for u in (0, 1):
                    b = 2 * i + u
                    pe.wait_ge(normed[1], b + 1)
                    transposes(bank[:, 4 * u, :], xn[:, u, :]).then_inc(xT_mm[1], 1)
                for u in (0, 1):
                    b = 2 * i + u
                    pe.wait_ge(x_new[1][u], i + 1)
                    pe.wait_ge(xT_low[1], b + 1)
                    for c in range(C):
                        last = mm3(bank[:, 4 * u + 1, :], [xT[:, u, w, c, :] for w in (0, 1)],
                                   [W0p[:, w, c, :] for w in (0, 1)], c == 0, c == C - 1)
                    last.then_inc(y_mm, 1)

            pe.wait_ge(raw_split, N_ATTN)
            pe.wait_ge(ready_bf, 2)
            pe.wait_ge(ones_set, 6)
            attn_rows = slice(0, STACK)

            def ahead_mm(pair, item, n):
                o = bank[:, AHEAD_BANK[item, n], :]
                if item == "x":
                    pe.wait_ge(normed[2], 2 * pair + n + 1)
                    transposes(o, xn[:, n, :]).then_inc(xT_mm[2], 1)
                elif item == "c":
                    pe.wait_ge(ctx_ld[n], 16 * pair + 16 * PAIRS + 16)
                    if n == 1:
                        pe.wait_ge(xT_low[2], 2 * pair + 1)
                    transposes(o, ctx_s[:, n, :]).then_inc(cT_mm[n], 1)
                elif item == "q":
                    pe.wait_ge(xT_low[2], 2 * pair + 2)
                    if n == 1:
                        pe.wait_ge(cT_low, 2 * pair + 1)
                    for j in (0, 1):
                        js = slice((2 * n + j) * P, (2 * n + j + 1) * P)
                        for c in range(C):
                            last = mm3(o[:, j * 2 * S:(j + 1) * 2 * S], [WQ[:, w, c, js] for w in (0, 1)],
                                       [xT3[:, c, w, :, :] for w in (0, 1)], c == 0, c == C - 1)
                    last.then_inc(q_mm, 1)
                elif item == "k":
                    pe.wait_ge(cT_low, 2 * pair + 2)
                    values_mm(o, 0)
                    for c in range(C):
                        last = mm3(o[:, 0:2 * S], [WK[:, w, c, :] for w in (0, 1)], [cT[:, c, w, :, :] for w in (0, 1)],
                                   c == 0, c == C - 1)
                    last.then_inc(k_mm, 1)
                elif item == "v":
                    pe.wait_ge(q_low, 2 * pair + 2)
                    values_mm(o, 1)

            def values_mm(o, u):
                for c in range(C):
                    last = mm3(o[:, (2 + u) * S:(3 + u) * S], [cT[:, c, w, u, :] for w in (0, 1)],
                               [WV[:, w, c, :] for w in (0, 1)], c == 0, c == C - 1)
                last.then_inc(v_mm, 1)

            def scores_for_max(i, u):
                b = 2 * i + u
                pe.wait_ge(stacked[u], 16 * 6 * i + 16 * 6)
                if u == 0:
                    pe.wait_ge(v_set, b + 2)
                for n in range(8):
                    half, r = n // 4, n % 4
                    o = bank[:, RING[n % 3], :]
                    if n >= 3:
                        pe.wait_ge(row_max, 8 * b + n - 2)
                    elif u == 1:
                        pe.wait_ge(row_max, 8 * b)
                    mm(o, ident_bf[:], never[:, 0, :].unsqueeze(1).broadcast_to([P, 4, S]), stop=False)
                    for jl in (0, 1):
                        j = 2 * half + jl
                        last = mm(o[:, jl * 256:(jl + 1) * 256], qst[0:TOP_ROW, u, r, j * P:(j + 1) * P],
                                  kst[0:TOP_ROW, u, r, :, :], False, jl == 1)
                    last.then_inc(score_mm, 1)

            def turned_maxima(i, u):
                b = 2 * i + u
                if u == 0:
                    pe.wait_ge(x_new[2][1], i + 1)
                else:
                    pe.wait_ge(mT_low, b)
                pe.wait_ge(row_max, 8 * b + 8)
                t.transpose(bank[0:HEADS, SPARE, 0:S], mx[:, u, :, :, :].rearrange("p e r j -> p (e r j)"), ident).then_inc(mT_mm, 1)

            def scores_less_max(i, s):
                u, g = s // GROUPS, s % GROUPS
                o = bank[:, LESS_RING[s % 2], :]
                if g == 0:
                    pe.wait_ge(maxima_in[u], 64 * i + 64)
                if s >= 2:
                    pe.wait_ge(probs, STEPS * i + s - 1)
                mm(o, ident_bf[:], never[:, 1, :].unsqueeze(1).broadcast_to([P, HPG, S]), stop=False)
                mm(o, kst[attn_rows, u, g // 2, g % 2, :], qst[attn_rows, u, g // 2, :], False, True).then_inc(less_mm, 1)

            def attend(i, s):
                u, g = s // GROUPS, s % GROUPS
                if u == 1 and g % 4 == 0:
                    pe.wait_ge(att_set, 4 * i + 1 + g // 4)
                pe.wait_ge(probs, STEPS * i + s + 1)
                for j in range(HPG):
                    at = (g % 4 * HPG + j) * VW
                    last = mm(bank[:, AV_BANK[g // 4], at:at + VW], ET[:, s % 4, j, :], vx[:, u, g, :])
                last.then_inc(av_mm, 1)

            def turned_attention(i, u):
                pe.wait_ge(att_set, 4 * i + 2 * u + 2)
                if u == 0:
                    pe.wait_ge(mT_low, 2 * i + 2)
                else:
                    pe.wait_ge(x_new[2][0], i + 2)
                transposes(bank[:, SPARE, :], att[:, u, :]).then_inc(aT_mm, 1)

            def output_projection(i, u):
                pe.wait_ge(aT_low, 2 * i + u + 1)
                for c in range(C):
                    last = mm3(bank[:, SPARE, :], [aT[:, u, w, c, :] for w in (0, 1)], [WO[:, w, c, :] for w in (0, 1)],
                               c == 0, c == C - 1)
                last.then_inc(o_mm, 1)

            def attention(i, ahead):
                for u in (0, 1):
                    scores_for_max(i, u)
                    turned_maxima(i, u)
                for s in range(STEPS):
                    scores_less_max(i, s)
                    if s >= 2:
                        attend(i, s - 2)
                    if ahead and s in AHEAD:
                        ahead_mm(i + 1, *AHEAD[s])
                    if s == 11:
                        turned_attention(i, 0)
                    if s == 14:
                        output_projection(i, 0)
                attend(i, STEPS - 2)
                attend(i, STEPS - 1)
                turned_attention(i, 1)
                output_projection(i, 1)

            for item in AHEAD.values():
                ahead_mm(0, *item)
            with pe.Fori(0, PAIRS - 1) as i:
                attention(i, True)
            attention(PAIRS - 1, False)

            pe.wait_ge(raw_split, len(staged))
            with pe.Fori(0, PAIRS) as i:
                for u in (0, 1):
                    b = 2 * i + u
                    pe.wait_ge(x_new[3][u], i + 1)
                    pe.wait_ge(normed[3], b + 1)
                    transposes(bank[:, 4 * u, :], xn[:, u, :]).then_inc(xT_mm[3], 1)
                for u in (0, 1):
                    b, k = 2 * i + u, 4 * u
                    pe.wait_ge(xT_low[3], b + 1)
                    x_parts = [[xT[:, u, w, c, :] for w in (0, 1)] for c in range(C)]
                    for c in range(C):
                        last = mm3(bank[:, k + 1, 0:EXPERTS], x_parts[c], [WR[:, w, c, :] for w in (0, 1)], c == 0, c == C - 1)
                    last.then_inc(r_mm, 1)
                    for q in (0, 1):
                        for c in range(C):
                            last = mm3(bank[:, k + 2 + q, :], x_parts[c], [MA[:, w, c, q * D:(q + 1) * D] for w in (0, 1)],
                                       c == 0, c == C - 1)
                        last.then_inc(h_mm, 1)
                for u in (0, 1):
                    b, k = 2 * i + u, 4 * u
                    hf = hg[u].rearrange("p k r -> p (k r)")
                    for q in (0, 1):
                        pe.wait_ge(hg_set, 2 * b + q + 1)
                        transposes(bank[:, k + q, :], hf[:, q * D:(q + 1) * D]).then_inc(hT_mm, 1)
                for u in (0, 1):
                    b, k = 2 * i + u, 4 * u
                    for c in range(KC):
                        if c % C == 0:
                            pe.wait_ge(hT_low, 2 * b + c // C + 1)
                        last = mm3(bank[:, k + 2, :], [hT[u][:, w, c, :] for w in (0, 1)], [MB[:, w, c, :] for w in (0, 1)],
                                   c == 0, c == KC - 1)
                    last.then_inc(e_mm, 1)


def kernel(x, ctx_4096, mask_SxS2_bk0, g_xattn, g_ffn, L0_ffn_lora_A, L0_ffn_lora_B, L0_ffn_W, L0_ffn_bias,
           L0_ffn_lora_weights, L1_xattn_w_q, L1_xattn_w_k, L1_xattn_w_v, L1_xattn_w_out, L1_ffn_A, L1_ffn_B,
           L1_ffn_Wr):
    import concourse.bacc as bacc
    from concourse.bass_utils import run_bass_kernel_spmd

    def rows_by_chunk(w):
        return w.reshape(-1, P, w.shape[-1]).transpose(1, 0, 2)

    asnp = np.asarray
    g_x, g_f = asnp(g_xattn), asnp(g_ffn)
    gates = np.broadcast_to(np.stack([g_x[0], g_f[0], g_x[1], g_f[1]]), (P, 4))
    wq = asnp(L1_xattn_w_q).reshape(GROUPS, HPG, DH, D).transpose(1, 0, 2, 3).reshape(D, D).T
    m = transform_matrices()
    rows, r = np.arange(P) // DH % 2, np.arange(P) - TOP_ROW
    arrays = {
        "x": asnp(x), "ctx": asnp(ctx_4096), "mask": asnp(mask_SxS2_bk0), "mask_t": asnp(mask_SxS2_bk0).T, "gates": gates,
        "w_base": rows_by_chunk(asnp(L0_ffn_W).T),
        "lora_a": asnp(L0_ffn_lora_A).reshape(P, D),
        "lora_b": asnp(L0_ffn_lora_B).transpose(0, 2, 1).reshape(P, D),
        "lora_w": np.repeat(asnp(L0_ffn_lora_weights), P // 8).reshape(P, 1),
        "bias": np.broadcast_to(asnp(L0_ffn_bias), (P, D)),
        "wq": rows_by_chunk(wq), "wk": rows_by_chunk(asnp(L1_xattn_w_k).T), "wv": rows_by_chunk(asnp(L1_xattn_w_v).T),
        "wo": rows_by_chunk(asnp(L1_xattn_w_out).T),
        "moe_a": rows_by_chunk(asnp(L1_ffn_A).reshape(KR, D).T),
        "moe_b": rows_by_chunk(asnp(L1_ffn_B).transpose(0, 2, 1).reshape(KR, D)),
        "w_router": rows_by_chunk(asnp(L1_ffn_Wr).T),
        "mats": np.stack([m[n] for n in MATS], 1).astype(np.float32),
        "parity": np.stack([rows == 0, rows == 1, r // 2 == 0, r // 2 == 1], 1).astype(np.float32),
    }
    nc = bacc.Bacc("TRN2", target_bir_lowering=False, num_devices=1)
    ins, args = {}, []
    for name, a in arrays.items():
        a = np.ascontiguousarray(a)
        ins[f"in_{name}"] = a
        args.append(nc.dram_tensor(f"in_{name}", a.shape, mybir.dt.from_np(a.dtype), kind="ExternalInput").ap())
    out = nc.dram_tensor("out", (B, S, D), F32, kind="ExternalOutput").ap()
    flamingo_kernel(nc, *args, out)
    r = run_bass_kernel_spmd(nc, [ins], core_ids=[0])
    return r.results[0]["out"]
```

```python
from contextlib import ExitStack

import numpy as np

import concourse.bass as bass
from concourse import mybir

F32 = mybir.dt.float32
BF16 = mybir.dt.bfloat16
F32R = mybir.dt.float32r
ALU = mybir.AluOpType
ACT = mybir.ActivationFunctionType
AX = mybir.AxisListType.X

B, S, D = 8, 128, 512
P = 128
C = D // P
PAIRS = B // 2
EPS = 1e-5

DELAYS = 9
TAKEN = -2.0 ** 127
HALF = S // 2
STAND_IN = -1.5 * 2.0 ** 127
FILL = 7

HEADS, GROUPS, DH = 32, 8, 16
HPG = HEADS // GROUPS
PAIRS_G = GROUPS // 2
VW = DH + 1
SLOTS = (0, 1, 0), (0, 0, 1)
TOP_ROW = 3 * 32
STACK = TOP_ROW + 4

EXPERTS, RANK = 64, 16
KR = EXPERTS * RANK
KC = KR // P

def transform_matrices():
    t = np.arange(S)
    r = np.arange(S)
    re = r <= HALF
    k = np.where(re, r, r - HALF)
    a = 2 * np.pi * np.outer(k, t) / S
    cos, sin = np.cos(a), np.sin(a)
    sin[HALF] = 0.0
    fa = np.where(re[:, None], cos, -sin)
    w = np.where((k == 0) | (k == HALF), 1.0, 2.0)[:, None] / S
    g1 = np.where(re[:, None], w * cos, -w * sin)
    g2 = np.where(re[:, None], w * sin, w * cos)
    h1 = 0.5 * np.where(re[:, None], w * cos, w * sin)
    h2 = 0.5 * np.where(re[:, None], -w * sin, w * cos)
    h2[0, :] = 0.5
    hr = r < HALF
    kk = np.where(hr, r, r - HALF) + 0.5
    o = 2 * np.pi * np.outer(kk, t) / S
    oc, os = np.cos(o), np.sin(o)
    less_last = np.eye(S)
    less_last[:, S - 1] -= 1.0
    fo = np.where(hr[:, None], oc, -os)
    j1 = (1.0 / S) * np.where(hr[:, None], oc, os)
    j2 = (1.0 / S) * np.where(hr[:, None], -os, oc)
    return {"FA": fa.T, "FL": (fo @ less_last).T, "FO": fo.T,
            "G1": g1, "G2": g2, "H1": h1, "H2": h2, "J1": j1, "J2": j2, "ID": np.eye(S)}


MATS = list(transform_matrices())


def flamingo_kernel(nc, x, ctx_in, mask, mask_t, gates, w_base, lora_a, lora_b, lora_w, bias, wq, wk, wv, wo,
                    moe_a, moe_b, w_router, mats, parity, out):
    with ExitStack() as st:
        def sb(name, shape, dt=F32):
            return st.enter_context(nc.sbuf_tensor(name, shape, dt))

        def sem(name):
            return st.enter_context(nc.semaphore(name))

        def sems(name):
            return [sem(f"{name}{u}") for u in (0, 1)]

        X = sb("X", [P, B, D])
        stats = sb("stats", [P, B, 2])
        rstd = sb("rstd", [P, B])
        ident = sb("ident", [P, P])[:]
        ident_bf = sb("ident_bf", [P, P], BF16)
        mask_u8 = sb("mask_u8", [P, 2, S], mybir.dt.uint8)
        never = sb("never", [P, 2, S], BF16)
        par = sb("par", [P, 4])
        g_in = sb("g_in", [P, 4])
        tg = sb("tg", [P, 4])
        WQ = sb("WQ", [P, 2, C, D], F32R)
        WK = sb("WK", [P, 2, C, P], F32R)
        WV = sb("WV", [P, 2, C, P], F32R)
        WO = sb("WO", [P, 2, C, D], F32R)
        raw = sb("raw", [P, 4 * D])
        zero_eps = sb("zero_eps", [P, 2])
        neg_half = sb("neg_half", [P, 1])
        ctx_s = sb("ctx_s", [P, 2, D])
        xn = sb("xn", [P, 2, D])
        bn = sb("bn", [P, 2, 6])
        mv = sb("mv", [P, 2, 2])
        tick = sb("tick", [P, 1])
        xT = sb("xT", [P, 2, 2, C, P], F32R)

        early = ExitStack()

        def sb1(name, shape, dt=F32):
            return early.enter_context(nc.sbuf_tensor(name, shape, dt))

        M = sb1("M", [P, len(MATS), S])
        mat = {n: M[:, k, :] for k, n in enumerate(MATS)}
        W0 = sb1("W0", [P, C, D])
        W0p = sb1("W0p", [P, 2, C, D], F32R)
        xT2 = sb1("xT2", [P, 2, 2, C, P], F32R)
        xn2 = sb1("xn2", [P, 2, D])
        LA = sb1("LA", [P, D])
        LB = sb1("LB", [P, D])
        lw = sb1("lw", [P, 2])
        BI = sb1("BI", [P, D])
        spectra = sb1("spectra", [P, 2, 4, D])
        x_spec = sb1("x_spec", [P, 2, D])
        raw_attn = [sb1(f"raw_attn{n}", [P, C, w])[:] for n, w in enumerate((D, P, P))]
        raw_attn += [raw.rearrange("p (c n) -> p c n", c=C)]
        products = sb1("products", [P, 2, 4, D])
        B1s, B2s, C1s, C2s = ([spectra[:, u, k, :] for u in (0, 1)] for k in range(4))
        spec = [[products[:, u, k, :] for k in range(4)] for u in (0, 1)]
        x_plus_bias = [spectra[:, u, 0, :] for u in (0, 1)]
        less = sb1("less", [P, 2, 2, C, S + FILL])
        expc = sb1("expc", [P, 2, C, S])
        kept = sb1("kept", [P, 2, C, S])
        wts = sb1("wts", [P, 2, C, S])
        wT = sb1("wT", [P, 2, D])
        top9 = sb1("top9", [P, 2, C, DELAYS])
        nxt = sb1("nxt", [P, 2, C, 8])
        ninth = sb1("ninth", [P, 2, C, 8])
        ntop = sb1("ntop", [P, 2, C])
        vals = sb1("vals", [P, 2, C, DELAYS])
        vsum = sb1("vsum", [P, 2, 2, C])
        early.close()

        MA = sb("MA", [P, 2, C, KR], F32R)
        MB = sb("MB", [P, 2, KC, D], F32R)
        WR = sb("WR", [P, 2, C, EXPERTS], F32R)
        cT = sb("cT", [P, C, 2, 2, P], F32R)
        qp = sb("qp", [P, 2, 2, HPG, S], F32R)
        kp = sb("kp", [P, 2, 2, 2, S], F32R)
        kf = sb("kf", [P, 2, 2, S])
        qst = sb("qst", [P, 2, PAIRS_G, D], F32R)
        kst = sb("kst", [P, 2, PAIRS_G, 2, S], F32R)
        vx = sb("vx", [P, 2, GROUPS, VW])
        xT3 = xT.rearrange("p u w c n -> p (u w c n)").rearrange("p (c w u n) -> p c w u n", c=C, w=2, u=2)
        att, aT = xn, xT
        ET = sb("ET", [P, 4, HPG, S])
        mx = sb("mx", [P, 2, 2, PAIRS_G, HPG])
        mT = sb("mT", [HEADS, 2, 2, S], F32R)
        iden = sb("iden", [P, 2, 4 * HPG])
        hg = [ET[:, 2 * u:2 * u + 2, :, :].rearrange("p a h (k r) -> p (a h k) r", r=RANK) for u in (0, 1)]
        hT = [qst[:, u, :, :].rearrange("p a (c n) -> p a c n", n=P).rearrange("p (w a) c n -> p w (a c) n", w=2) for u in (0, 1)]
        rl = ctx_s[:, :, 0:2 * EXPERTS].rearrange("p u (k e) -> p u k e", k=2)
        re, rk, G = (ctx_s[:, :, k * EXPERTS:(k + 1) * EXPERTS] for k in (2, 3, 4))
        rt = ctx_s[:, :, 5 * EXPERTS:5 * EXPERTS + 16].rearrange("p u (k e) -> p u k e", k=2)
        rs = ctx_s[:, :, 5 * EXPERTS + 16:5 * EXPERTS + 20]

        q_turn = nc.dram_tensor("q_turn", (P, 2, 2, HPG * S), F32, kind="Internal").ap()
        k_turn = nc.dram_tensor("k_turn", (P, 2, 2, 2 * S), F32, kind="Internal").ap()

        bank = st.enter_context(nc.psum_tensor("bank", [P, 8, D], F32))

        x_in, ctx_ld = [sem(f"x_in{b}") for b in range(B)], sems("ctx_ld")
        mats_in, rest_in, gate_in, mask_in, lora_in = (sem(n) for n in ("mats_in", "rest_in", "gate_in", "mask_in", "lora_in"))
        attn_in, attn_high, x_spec_out = sem("attn_in"), sem("attn_high"), sem("x_spec_out")
        raw_in, raw_scaled, raw_high, raw_split = (sem(n) for n in ("raw_in", "raw_scaled", "raw_high", "raw_split"))
        consts_set, tanh_done, scaled = sem("consts_set"), sem("tanh_done"), sem("scaled")
        ready_bf = sem("ready_bf")
        bn_done = [sem(f"bn_done{p}") for p in range(4)]
        mv_done = [sem(f"mv_done{p}") for p in range(4)]
        stats_done = [sem(f"stats_done{p}") for p in range(4)]
        rstd_done = [sem(f"rstd_done{p}") for p in range(4)]
        normed = [sem(f"normed{p}") for p in range(4)]
        x_new = [sems(f"x_new{p}_") for p in range(4)]

        a_mm, cyc_mm, cT_mm = sem("a_mm"), sem("cyc_mm"), sems("cT_mm")
        half_mm, cyc_twice, half_twice = sems("half_mm"), sems("cyc_twice"), sems("half_twice")
        cyc_out, half_out = sem("cyc_out"), sem("half_out")
        corr_prod, corr_mm = sem("corr_prod"), sem("corr_mm")
        top8, neg_top, less8, next8, ninth_set = (sem(n) for n in ("top8", "neg_top", "less8", "next8", "ninth_set"))
        less9, kept_mask, vals_sub, vals_exp = (sem(n) for n in ("less9", "kept_mask", "vals_sub", "vals_exp"))
        exp_c, vals_sum, inv_sum, w_built = (sem(n) for n in ("exp_c", "vals_sum", "inv_sum", "w_built"))
        wt_mm, wt_out, we_mm, wo_mm, spec_prod, inv_mm = (
            sem(n) for n in ("wt_mm", "wt_out", "we_mm", "wo_mm", "spec_prod", "inv_mm"))

        lora_mm, lora_folded, w0_high, w0_low = (sem(n) for n in ("lora_mm", "lora_folded", "w0_high", "w0_low"))
        x_bias = sem("x_bias")
        xT_mm = [sem(f"xT_mm{p}") for p in range(4)]
        xT_high = [sem(f"xT_high{p}") for p in range(4)]
        xT_low = [sem(f"xT_low{p}") for p in range(4)]
        y_mm = sem("y_mm")

        cT_high, cT_low, q_mm, q_high, q_low, k_mm, v_mm, k_set, k_high, k_low, v_set = (
            sem(n) for n in ("cT_high", "cT_low", "q_mm", "q_high", "q_low", "k_mm", "v_mm", "k_set", "k_high", "k_low", "v_set"))
        ones_set = sem("ones_set")
        stacked, maxima_in = sems("stacked"), sems("maxima_in")
        q_away, k_away = sem("q_away"), sem("k_away")
        score_mm, row_max, mT_mm, mT_high, mT_low = (sem(n) for n in ("score_mm", "row_max", "mT_mm", "mT_high", "mT_low"))
        less_mm, probs, av_mm = (sem(n) for n in ("less_mm", "probs", "av_mm"))
        inv_den, att_set, aT_mm, aT_high, aT_low, o_mm = (
            sem(n) for n in ("inv_den", "att_set", "aT_mm", "aT_high", "aT_low", "o_mm"))

        r_mm, h_mm, r_top, r_less, r_top2, r_less2, r_neg, r_exp, r_kept, r_sum, r_inv, gate_set = (
            sem(n) for n in ("r_mm", "h_mm", "r_top", "r_less", "r_top2", "r_less2", "r_neg", "r_exp",
                             "r_kept", "r_sum", "r_inv", "gate_set"))
        hg_set, hT_mm, hT_high, hT_low, e_mm, stored = (
            sem(n) for n in ("hg_set", "hT_mm", "hT_high", "hT_low", "e_mm", "stored"))

        attn_weights = (wq, WQ), (wk, WK), (wv, WV), (wo, WO)
        N_ATTN = len(attn_weights)
        staged = [(w_router, WR, None, 1.0)]
        staged += [(moe_a[:, c:c + 2, :], MA[:, :, c:c + 2, :], None, 1.0) for c in range(0, C, 2)]
        staged += [(moe_b[:, c:c + 4, :], MB[:, :, c:c + 4, :], 3, 2.0) for c in range(0, KC, 4)]

        FIRST = {4: (("c", 0), ("c", 1), ("x", 0), ("x", 1)), 5: (("k", 0), ("q", 0), ("q", 1)), 6: (("v", 1),), 7: ()}

        LORA_BANK = 3, 1, 2, 3
        RING, INPUT_BANK, LESS_RING, AV_BANK, SPARE = (0, 1), 2, (3, 4), (5, 6), 7
        TURNED_MAX = INPUT_BANK, SPARE
        STEPS = 2 * GROUPS
        MAX_BANKS = 8
        MAX_RING = *RING, *LESS_RING
        MAX_FIRST = 4
        MAX_STEPS = 0, 1
        MAX_TURN = 3

        def max_bank(u, n):
            if u == 0 or n < MAX_FIRST:
                return bank[:, MAX_RING[n % 4], :]
            return bank[:, RING[n % 2], :]

        AHEAD = {1: ("c", 0), 3: ("x", 0), 4: ("c", 1), 5: ("x", 1), 7: ("q", 0), 9: ("q", 1), 11: ("k", 0), 13: ("v", 1)}
        AHEAD_BANK = {("x", 0): INPUT_BANK, ("x", 1): INPUT_BANK, ("c", 0): INPUT_BANK, ("c", 1): INPUT_BANK,
                      ("q", 0): RING[0], ("q", 1): RING[1], ("k", 0): INPUT_BANK, ("v", 1): RING[1]}
        FIRST_BANK = {**AHEAD_BANK, ("c", 1): RING[1], ("x", 0): RING[0], ("x", 1): LESS_RING[0]}

        def input_bank(pair, item, n):
            first = isinstance(pair, int) and pair == 0
            return bank[:, (FIRST_BANK if first else AHEAD_BANK)[item, n], :]

        block = st.enter_context(nc.Block())

        @block.sync
        def _(sp):
            for u in (0, 1):
                for p in range(4):
                    sp.sem_inc(x_new[p][u], 1)
            sp.dma_start(M[:, 0:2, :], mats[:, 0:2, :]).then_inc(mats_in, 16)
            for u in (0, 1):
                sp.dma_start(ctx_s[:, u, :], ctx_in[u]).then_inc(ctx_ld[u], 16)
                sp.dma_start(X[:, u, :], x[u]).then_inc(x_in[u], 16)
            sp.dma_start(M[:, 2:, :], mats[:, 2:, :]).then_inc(rest_in, 16)

            def both_halves(b, u):
                sp.wait_ge(cyc_out, 2 * b + 2)
                sp.dma_start(B1s[u][HALF + 1:S], B1s[u][1:HALF]).then_inc(cyc_twice[u], 16)
                sp.dma_start(B2s[u][1:HALF], B2s[u][HALF + 1:S]).then_inc(cyc_twice[u], 16)
                sp.dma_start(B2s[u][0:1], ctx_in[b, S - 1:S]).then_inc(cyc_twice[u], 16)
                sp.wait_ge(half_out, 2 * b + 2)
                sp.dma_start(C1s[u][HALF:S], C1s[u][0:HALF]).then_inc(half_twice[u], 16)
                sp.dma_start(C2s[u][0:HALF], C2s[u][HALF:S]).then_inc(half_twice[u], 16)

            both_halves(0, 0)
            sp.dma_start(X[:, 2, :], x[2]).then_inc(x_in[2], 16)
            both_halves(1, 1)
            for b in range(3, B):
                sp.dma_start(X[:, b, :], x[b]).then_inc(x_in[b], 16)
            for tile, src in (W0, w_base), (LA, lora_a), (LB, lora_b), (lw[:, 0:1], lora_w), (BI, bias):
                sp.dma_start(tile[:], src).then_inc(lora_in, 16)
            for tile, src in (mask_u8[:, 0, :], mask), (mask_u8[:, 1, :], mask_t), (par[:], parity):
                sp.dma_start(tile, src).then_inc(mask_in, 16)
            with sp.Fori(0, PAIRS - 1) as i:
                for u in (0, 1):
                    sp.dma_start(ctx_s[:, u, :], ctx_in[2 * i + u + 2]).then_inc(ctx_ld[u], 16)
                for u in (0, 1):
                    both_halves(2 * i + u + 2, u)
            for u in (0, 1):
                sp.dma_start(ctx_s[:, u, :], ctx_in[u]).then_inc(ctx_ld[u], 16)

            def stack(pair, after_group):
                def keys_away():
                    sp.wait_ge(k_low, pair + 1)
                    sp.dma_start(k_turn, kp[:].rearrange("p w u e n -> p w u (e n)").bitcast(F32)).then_inc(k_away, 16)

                if not after_group:
                    keys_away()
                sp.wait_ge(q_low, 2 * pair + 2)
                sp.dma_start(q_turn, qp[:].rearrange("p w u j n -> p w u (j n)").bitcast(F32)).then_inc(q_away, 16)
                if after_group:
                    keys_away()
                sp.wait_ge(q_away, 16 * pair + 16)
                for u in (0, 1):
                    if after_group:
                        after_group(u)
                    for slot, part in enumerate(SLOTS[0]):
                        sp.dma_start(qst[32 * slot:32 * slot + 32, u, :, :].bitcast(F32),
                                     q_turn.rearrange("(r p) w u n -> w u p r n", p=32)[part, u]).then_inc(stacked[u], 16)
                    if u == 0:
                        sp.wait_ge(k_away, 16 * pair + 16)
                    for slot, part in enumerate(SLOTS[1]):
                        sp.dma_start(kst[32 * slot:32 * slot + 32, u, :, :, :].rearrange("p r e n -> p r (e n)").bitcast(F32),
                                     k_turn.rearrange("(r p) w u n -> w u p r n", p=32)[part, u]).then_inc(stacked[u], 16)

            def maxima(i, u):
                sp.wait_ge(mT_low, 2 * i + u + 1)
                for e in (0, 1):
                    for part in (0, 1):
                        row = TOP_ROW + 2 * e + part
                        sp.dma_start(qst[row:row + 1, u, :, :].rearrange("p r (j n) -> p (r j) n", j=HPG).bitcast(F32),
                                     mT[16 * e:16 * e + 16, u, part, :].bitcast(F32)).then_inc(maxima_in[u], 16)

            stack(0, None)
            maxima(0, 0)
            with sp.Fori(0, PAIRS - 1) as i:
                for u in (0, 1):
                    sp.wait_ge(cT_mm[u], i + 1)
                    sp.dma_start(ctx_s[:, u, :], ctx_in[2 * i + u + 2]).then_inc(ctx_ld[u], 16)
                maxima(i, 1)
                stack(i + 1, lambda u: sp.wait_ge(less_mm, STEPS * i + GROUPS * (u + 1)))
                maxima(i + 1, 0)
            maxima(PAIRS - 1, 1)
            with sp.Fori(0, PAIRS) as i:
                for u in (0, 1):
                    sp.wait_ge(x_new[3][u], i + 2)
                    sp.dma_start(out[2 * i + u], X[:, 2 * i + u, :]).then_inc(stored, 16)
            sp.wait_ge(stored, 16 * B)

        @block.gpsimd
        def _(pool):
            g = nc.gpsimd
            g.memset(zero_eps[:, 0:1], 0.0).then_inc(consts_set, 1)
            g.memset(zero_eps[:, 1:2], EPS).then_inc(consts_set, 1)
            g.memset(neg_half[:], -0.5).then_inc(consts_set, 1)
            g.memset(less[:], STAND_IN).then_inc(consts_set, 1)
            g.memset(ninth[:], STAND_IN).then_inc(consts_set, 1)
            pool.wait_ge(consts_set, 5)

            def inverse_std(p, b, u):
                pool.wait_ge(stats_done[p], b + 1)
                pool.wait_ge(consts_set, 5)
                g.tensor_tensor(rstd[:, bass.ds(b, 1)], stats[:, b, 1:2], neg_half[:], ALU.pow).then_inc(rstd_done[p], 1)

            def correlation_products(b, u, i):
                pool.wait_ge(x_spec_out, b + 1)
                pool.wait_ge(cyc_twice[u], 48 * i + 48)
                for n, Bs in enumerate((B1s[u], B2s[u])):
                    g.tensor_tensor(spec[u][n], x_spec[:, u, :], Bs, ALU.mult).then_inc(corr_prod, 1)

            for b in (0, 1):
                inverse_std(0, b, b)
            correlation_products(0, 0, 0)
            correlation_products(1, 1, 0)
            for b in range(2, B):
                inverse_std(0, b, b % 2)
            for n, (src, _) in enumerate(attn_weights):
                pool.dma_start(raw_attn[n], src).then_inc(attn_in, 16)

            def split(n):
                src, parts, gate, factor = staged[n]
                w = raw[:, 0:src.shape[1] * src.shape[2]].rearrange("p (c n) -> p c n", c=src.shape[1])
                if n:
                    pool.wait_ge(raw_split, N_ATTN + n)
                pool.dma_start(w, src).then_inc(raw_in, 16)
                scales = sum(x[2] is not None for x in staged[:n])
                pool.wait_ge(raw_in, 16 * (n + 1))
                if gate is not None:
                    g.tensor_scalar(w, w, tg[:, gate:gate + 1], factor, ALU.mult, ALU.mult).then_inc(raw_scaled, 1)
                    pool.wait_ge(raw_scaled, scales + 1)
                g.tensor_copy(parts[:, 0], w).then_inc(raw_high, 1)
                pool.wait_ge(raw_high, n + 1)
                g.tensor_tensor(parts[:, 1], w, parts[:, 0].bitcast(F32), ALU.subtract).then_inc(raw_split, 1)

            pool.wait_ge(tanh_done, 1)
            pool.wait_ge(lora_in, 16 * 5)
            g.tensor_scalar(lw[:, 1:2], lw[:, 0:1], tg[:, 1:2], 2.0, ALU.mult, ALU.mult).then_inc(scaled, 1)
            pool.wait_ge(scaled, 1)
            g.tensor_scalar(LB[:], LB[:], lw[:, 1:2], 1.0, ALU.mult, ALU.mult).then_inc(scaled, 1)
            g.tensor_scalar(W0[:], W0[:], tg[:, 1:2], 1.0, ALU.mult, ALU.mult).then_inc(scaled, 1)
            g.tensor_scalar(BI[:], BI[:], tg[:, 1:2], 1.0, ALU.mult, ALU.mult).then_inc(scaled, 1)

            with pool.Fori(0, PAIRS - 1) as i:
                for u in (0, 1):
                    b = 2 * i + u
                    pool.wait_ge(inv_mm, b + 1)
                    correlation_products(b + 2, u, i + 1)
                    inverse_std(1, b, u)
            pool.wait_ge(attn_in, 16 * N_ATTN)
            g.tensor_scalar(raw_attn[3], raw_attn[3], tg[:, 2:3], 1.0, ALU.mult, ALU.mult).then_inc(scaled, 1)
            for n, (_, parts) in enumerate(attn_weights):
                pool.wait_ge(attn_high, n + 1)
                g.tensor_tensor(parts[:, 1], raw_attn[n], parts[:, 0].bitcast(F32), ALU.subtract).then_inc(raw_split, 1)
            inverse_std(1, B - 2, 0)
            for c in range(C):
                pool.wait_ge(w0_high, c + 1)
                g.tensor_tensor(W0p[:, 1, c, :], W0[:, c, :], W0p[:, 0, c, :].bitcast(F32), ALU.subtract).then_inc(w0_low, 1)
            inverse_std(1, B - 1, 1)
            pool.wait_ge(scaled, 4)
            pool.wait_ge(x_new[0][0], PAIRS + 1)
            pool.wait_ge(x_new[0][1], PAIRS + 1)
            with pool.Fori(0, PAIRS) as i:
                for u in (0, 1):
                    pool.wait_ge(x_new[1][u], i + 1)
                    pool.wait_ge(consts_set, 5)
                    g.tensor_tensor(x_plus_bias[u], X[:, 2 * i + u, :], BI[:], ALU.add).then_inc(x_bias, 1)
                for u in (0, 1):
                    inverse_std(2, 2 * i + u, u)
            for u in (0, 1):
                pool.wait_ge(x_new[1][u], PAIRS + 1)
            for n in range(len(staged)):
                split(n)
            with pool.Fori(0, PAIRS) as i:
                for u in (0, 1):
                    inverse_std(3, 2 * i + u, u)

        @block.scalar
        def _(act):
            a = nc.scalar
            act.dma_start(g_in[:], gates).then_inc(gate_in, 16)
            act.dma_start(ident, mats[:, MATS.index("ID"), :]).then_inc(rest_in, 16)
            act.wait_ge(gate_in, 16)
            a.activation(tg[:], g_in[:], ACT.Tanh).then_inc(tanh_done, 1)

            def copy(dst, src):
                return a.activation(dst, src, ACT.Copy)

            def spectra_out(b, u, i):
                k = 4 * u
                act.wait_ge(cyc_mm, b + 1)
                copy(B1s[u][0:HALF + 1], bank[0:HALF + 1, k + 3, :]).then_inc(cyc_out, 1)
                copy(B2s[u][HALF:S], bank[HALF:S, k + 3, :]).then_inc(cyc_out, 1)
                act.wait_ge(half_mm[u], i + 1)
                copy(C1s[u][0:HALF], bank[0:HALF, k + 1, :]).then_inc(half_out, 1)
                copy(C2s[u][HALF:S], bank[HALF:S, k + 1, :]).then_inc(half_out, 1)
                act.wait_ge(a_mm, b + 1)
                copy(x_spec[:, u, :], bank[:, k + 2, :]).then_inc(x_spec_out, 1)

            def weights(b, u):
                k = 4 * u
                act.wait_ge(neg_top, b + 1)
                act.wait_ge(less8, C * b + C)
                for c in range(C):
                    a.activation(expc[:, u, c, :], bank[:, k + 0, c * S:(c + 1) * S], ACT.Exp,
                                 bias=ntop[:, u, c:c + 1]).then_inc(exp_c, 1)
                act.wait_ge(vals_sub, b + 1)
                a.activation(vals[:, u, :, :], vals[:, u, :, :], ACT.Exp).then_inc(vals_exp, 1)

            def weights_turned(b, u):
                act.wait_ge(wt_mm, b + 1)
                copy(wT[:, u, :], bank[:, 4 * u + 2, :]).then_inc(wt_out, 1)

            for u in (0, 1):
                spectra_out(u, u, 0)
            weights(0, 0)
            with act.Fori(0, PAIRS - 1) as i:
                for u in (0, 1):
                    b = 2 * i + u
                    weights_turned(b, u)
                    spectra_out(b + 2, u, i + 1)
                    weights(b + 1, 1 - u)
            weights_turned(B - 2, 0)
            act.wait_ge(scaled, 5)
            for n, (_, parts) in enumerate(attn_weights):
                copy(parts[:, 0], raw_attn[n]).then_inc(attn_high, 1)
            weights(B - 1, 1)
            weights_turned(B - 1, 1)

            for c in range(C):
                act.wait_ge(lora_folded, c + 1)
                copy(W0p[:, 0, c, :], W0[:, c, :]).then_inc(w0_high, 1)
            def ahead_high(pair, item, n):
                o = input_bank(pair, item, n)
                if item == "x":
                    act.wait_ge(xT_mm[2], 2 * pair + n + 1)
                    copy(xT3[:, :, 0, n, :], o.rearrange("p (c n) -> p c n", c=C)).then_inc(xT_high[2], 1)
                elif item == "c":
                    act.wait_ge(cT_mm[n], pair + 1)
                    copy(cT[:, :, 0, n, :], o.rearrange("p (c n) -> p c n", c=C)).then_inc(cT_high, 1)
                elif item == "q":
                    act.wait_ge(q_mm, 2 * pair + n + 1)
                    for u in (0, 1):
                        copy(qp[:, 0, u, 2 * n:2 * n + 2, :],
                             o.rearrange("p (j u n) -> p j u n", j=2, u=2)[:, :, u, :]).then_inc(q_high, 1)
                elif item == "k":
                    act.wait_ge(k_set, 2 * pair + 2)
                    copy(kp[:, 0, :, :, :], kf[:]).then_inc(k_high, 1)

            def turned_high(b, u):
                act.wait_ge(xT_mm[1], b + 1)
                copy(xT2[:, u, 0, :, :], bank[:, 6 + u, :]).then_inc(xT_high[1], 1)

            turned_high(0, 0)
            with act.Fori(0, PAIRS // 2) as i:
                for u in (0, 1):
                    turned_high(2 * i + u + 1, 1 - u)
            for b in range(B // 2, B):
                if b + 1 < B:
                    turned_high(b + 1, 1 - b % 2)
                for item in FIRST[b]:
                    ahead_high(0, *item)

            def experts_high(b, u):
                act.wait_ge(xT_mm[3], b + 1)
                copy(xT[:, u, 0, :, :], bank[:, 4 * u, :]).then_inc(xT_high[3], 1)

            def router_exp(b, u):
                act.wait_ge(r_neg, b + 1)
                act.wait_ge(r_less, b + 1)
                a.activation(re[:, u, :], bank[:, 4 * u + 1, 0:EXPERTS], ACT.Exp, bias=rs[:, u, 0:1]).then_inc(r_exp, 1)

            def minus_maxima(i, u):
                act.wait_ge(mT_mm, 2 * i + u + 1)
                a.activation(mT[:, u, 0, :], bank[0:HEADS, TURNED_MAX[u], 0:S], ACT.Copy, scale=-1.0).then_inc(mT_high, 1)

            def attention(i, ahead):
                for s in range(STEPS):
                    if s >= 4:
                        act.wait_ge(av_mm, STEPS * i + s - 3)
                    act.wait_ge(less_mm, STEPS * i + s + 1)
                    a.activation(ET[:, s % 4, :, :], bank[:, LESS_RING[s % 2], :], ACT.Exp,
                                 scale=DH ** -0.5).then_inc(probs, 1)
                    if s == MAX_TURN:
                        minus_maxima(i, 1)
                    if ahead and s in AHEAD:
                        ahead_high(i + 1, *AHEAD[s])
                    if s == 12:
                        act.wait_ge(aT_mm, 2 * i + 1)
                        copy(aT[:, 0, 0, :, :], bank[:, SPARE, :]).then_inc(aT_high, 1)
                if not ahead:
                    experts_high(0, 0)
                act.wait_ge(aT_mm, 2 * i + 2)
                copy(aT[:, 1, 0, :, :], bank[:, SPARE, :]).then_inc(aT_high, 1)
                if ahead:
                    minus_maxima(i + 1, 0)
                else:
                    router_exp(0, 0)
                    experts_high(1, 1)

            minus_maxima(0, 0)
            with act.Fori(0, PAIRS - 1) as i:
                attention(i, True)
            attention(PAIRS - 1, False)

            def turned_gated_high(b, u):
                for q in (0, 1):
                    act.wait_ge(hT_mm, 2 * b + q + 1)
                    copy(hT[u][:, 0, 4 * q:4 * q + 4, :], bank[:, 4 * u + q, :]).then_inc(hT_high, 1)

            with act.Fori(0, PAIRS - 1) as i:
                for u in (0, 1):
                    b = 2 * i + u
                    turned_gated_high(b, u)
                    router_exp(b + 1, 1 - u)
                    experts_high(b + 2, u)
            turned_gated_high(B - 2, 0)
            router_exp(B - 1, 1)
            turned_gated_high(B - 1, 1)

        @block.vector
        def _(dve):
            v = nc.vector

            def settle():
                v.memset(tick[:], 0.0)

            def token_stats(p, b, u):
                settle()
                v.bn_stats(bn[:, u, :], X[:, b, :]).then_inc(bn_done[p], 1)
                dve.wait_ge(bn_done[p], b + 1)
                settle()
                v.bn_aggr(mv[:, u, :], bn[:, u, :]).then_inc(mv_done[p], 1)
                dve.wait_ge(mv_done[p], b + 1)
                v.tensor_tensor(stats[:, b, :], mv[:, u, :], zero_eps[:], ALU.add).then_inc(stats_done[p], 1)

            def low(dst, whole, high):
                return v.tensor_tensor(dst, whole, high.bitcast(F32), ALU.subtract)

            def normalise(p, b, u):
                dve.wait_ge(rstd_done[p], b + 1)
                v.tensor_scalar((xn2 if p == 1 else xn)[:, u, :], X[:, b, :], stats[:, b, 0:1], rstd[:, bass.ds(b, 1)],
                                ALU.subtract, ALU.mult).then_inc(normed[p], 1)

            dve.wait_ge(consts_set, 5)
            def first_stats(b):
                dve.wait_ge(x_in[b], 16)
                v.bn_stats(bn[:, b % 2, :], X[:, b, :]).then_inc(bn_done[0], 1)
                dve.wait_ge(bn_done[0], b + 1)
                v.bn_aggr(mv[:, b % 2, :], bn[:, b % 2, :]).then_inc(mv_done[0], 1)
                dve.wait_ge(mv_done[0], b + 1)
                v.tensor_tensor(stats[:, b, :], mv[:, b % 2, :], zero_eps[:], ALU.add).then_inc(stats_done[0], 1)

            def pick_nine(b, u):
                corr = bank[:, 4 * u, :].rearrange("p (c s) -> p c s", c=C)
                dve.wait_ge(corr_mm, b + 1)
                settle()
                for c in range(C):
                    v.max(top9[:, u, c, 0:8], corr[:, c, :]).then_inc(top8, 1)
                dve.wait_ge(top8, C * b + C)
                v.tensor_scalar(ntop[:, u, :], top9[:, u, :, 0], -1.0, None, ALU.mult).then_inc(neg_top, 1)
                for c in range(C):
                    v.match_replace(less[:, u, 0, c, 0:S], top9[:, u, c, 0:8], corr[:, c, :], TAKEN).then_inc(less8, 1)
                dve.wait_ge(less8, C * b + C)
                settle()
                for c in range(C):
                    v.max(nxt[:, u, c, :], less[:, u, 0, c, 0:S]).then_inc(next8, 1)
                dve.wait_ge(next8, C * b + C)
                v.tensor_copy(ninth[:, u, :, 0], nxt[:, u, :, 0]).then_inc(ninth_set, 1)
                v.tensor_copy(top9[:, u, :, 8], nxt[:, u, :, 0]).then_inc(ninth_set, 1)
                dve.wait_ge(ninth_set, 2 * b + 2)
                v.tensor_tensor(vals[:, u, :, :], top9[:, u, :, :],
                                ntop[:, u, :].unsqueeze(2).broadcast_to([P, C, DELAYS]), ALU.add).then_inc(vals_sub, 1)

            def delay_weights(b, u):
                dve.wait_ge(vals_sub, b + 1)
                settle()
                for c in range(C):
                    v.match_replace(less[:, u, 1, c, :], ninth[:, u, c, :], less[:, u, 0, c, :], TAKEN).then_inc(less9, 1)
                dve.wait_ge(less9, C * b + C)
                v.tensor_scalar(kept[:, u, :, :], less[:, u, 1, :, 0:S], TAKEN, None, ALU.is_equal).then_inc(kept_mask, 1)
                dve.wait_ge(vals_exp, b + 1)
                v.reduce_sum(vsum[:, u, 0, :], vals[:, u, :, :], AX).then_inc(vals_sum, 1)
                dve.wait_ge(vals_sum, b + 1)
                v.reciprocal(vsum[:, u, 1, :], vsum[:, u, 0, :]).then_inc(inv_sum, 1)
                dve.wait_ge(inv_sum, b + 1)
                dve.wait_ge(kept_mask, b + 1)
                dve.wait_ge(exp_c, C * b + C)
                for c in range(C):
                    v.scalar_tensor_tensor(wts[:, u, c, :], expc[:, u, c, :], vsum[:, u, 1, c:c + 1],
                                           kept[:, u, c, :], ALU.mult, ALU.mult).then_inc(w_built, 1)

            def delay_products(b, u, i):
                k = 4 * u
                dve.wait_ge(we_mm, b + 1)
                v.tensor_tensor(spec[u][0], bank[:, k + 3, :], B1s[u], ALU.mult).then_inc(spec_prod, 1)
                v.tensor_tensor(spec[u][1], bank[:, k + 3, :], B2s[u], ALU.mult).then_inc(spec_prod, 1)
                dve.wait_ge(wo_mm, b + 1)
                dve.wait_ge(half_twice[u], 32 * i + 32)
                v.tensor_tensor(spec[u][2], bank[:, k + 1, :], C1s[u], ALU.mult).then_inc(spec_prod, 1)
                v.tensor_tensor(spec[u][3], bank[:, k + 1, :], C2s[u], ALU.mult).then_inc(spec_prod, 1)

            def add_delayed(b, u, i):
                dve.wait_ge(inv_mm, b + 1)
                v.scalar_tensor_tensor(X[:, b, :], bank[:, 4 * u, :], tg[:, 0:1], X[:, b, :],
                                       ALU.mult, ALU.add).then_inc(x_new[0][u], 1)
                dve.wait_ge(x_new[0][u], i + 2)
                token_stats(1, b, u)

            def correlate_step(b, u, i, last_steps=False):
                if not last_steps:
                    normalise(0, b + 2, u)
                delay_products(b, u, i)
                pick_nine(b + 1, 1 - u)
                delay_weights(b + 1, 1 - u)
                add_delayed(b, u, i)

            for b in (0, 1):
                first_stats(b)
            for u in (0, 1):
                normalise(0, u, u)
            pick_nine(0, 0)
            first_stats(2)
            delay_weights(0, 0)
            for b in range(3, B):
                first_stats(b)
            with dve.Fori(0, PAIRS - 1) as i:
                for u in (0, 1):
                    correlate_step(2 * i + u, u, i)
            correlate_step(B - 2, 0, PAIRS - 1, last_steps=True)
            def fold(c):
                dve.wait_ge(scaled, 3)
                dve.wait_ge(lora_mm, c + 1)
                v.tensor_tensor(W0[:, c, :], bank[:, LORA_BANK[c], :], W0[:, c, :], ALU.add).then_inc(lora_folded, 1)

            for c in range(C - 1):
                fold(c)
            for u in (0, 1):
                normalise(1, u, u)
            delay_products(B - 1, 1, PAIRS - 1)
            fold(C - 1)
            add_delayed(B - 1, 1, PAIRS - 1)
            dve.wait_ge(rest_in, 32)
            v.tensor_copy(ident_bf[:], ident).then_inc(ready_bf, 1)
            dve.wait_ge(mask_in, 48)
            v.tensor_scalar(never[:], mask_u8[:], 0.0, TAKEN, ALU.is_equal, ALU.mult).then_inc(ready_bf, 1)

            def turned_low(b, u):
                dve.wait_ge(xT_high[1], b + 1)
                low(xT2[:, u, 1, :, :], bank[:, 6 + u, :], xT2[:, u, 0, :, :]).then_inc(xT_low[1], 1)

            def add_feed_forward(b, u, i):
                dve.wait_ge(x_bias, b + 1)
                dve.wait_ge(y_mm, b + 1)
                v.tensor_tensor(X[:, b, :], bank[:, 4 + u, :], x_plus_bias[u], ALU.add).then_inc(x_new[1][u], 1)
                dve.wait_ge(x_new[1][u], i + 2)
                token_stats(2, b, u)

            def ahead_low(pair, item, n):
                o = input_bank(pair, item, n)
                if item == "x":
                    dve.wait_ge(xT_high[2], 2 * pair + n + 1)
                    low(xT3[:, :, 1, n, :], o.rearrange("p (c n) -> p c n", c=C), xT3[:, :, 0, n, :]).then_inc(xT_low[2], 1)
                elif item == "c":
                    dve.wait_ge(cT_high, 2 * pair + n + 1)
                    low(cT[:, :, 1, n, :], o.rearrange("p (c n) -> p c n", c=C), cT[:, :, 0, n, :]).then_inc(cT_low, 1)
                elif item == "q":
                    dve.wait_ge(q_high, 4 * pair + 2 * n + 2)
                    js = slice(2 * n, 2 * n + 2)
                    for u in (0, 1):
                        last = low(qp[:, 1, u, js, :], o.rearrange("p (j u n) -> p j u n", j=2, u=2)[:, :, u, :],
                                   qp[:, 0, u, js, :])
                    last.then_inc(q_low, 1)
                elif item == "k":
                    dve.wait_ge(k_mm, pair + 1)
                    for e in (0, 1):
                        v.tensor_scalar(kf[:, :, e, :], o[:, 0:2 * S].rearrange("p (u n) -> p u n", u=2), par[:, e:e + 1], None,
                                        ALU.mult).then_inc(k_set, 1)
                    values(pair, 0)
                    dve.wait_ge(k_high, pair + 1)
                    low(kp[:, 1, :, :, :], kf[:], kp[:, 0, :, :, :]).then_inc(k_low, 1)

            def values(pair, u):
                dve.wait_ge(v_mm, 2 * pair + u + 1)
                v.tensor_copy(vx[:, u, :, 0:DH], bank[:, AHEAD_BANK["kv"[u], u], (2 + u) * S:(3 + u) * S]
                              .rearrange("p (g w) -> p g w", w=DH)).then_inc(v_set, 1)

            turned_low(0, 0)
            for u in (0, 1):
                v.memset(vx[:, u, :, DH:VW], 1.0).then_inc(ones_set, 1)
                for e in (0, 1):
                    rows = slice(TOP_ROW, STACK)
                    v.tensor_copy(kst[rows, u, :, e, :],
                                  par[rows, 2 + e:3 + e].unsqueeze(2).broadcast_to([4, PAIRS_G, S])).then_inc(ones_set, 1)

            with dve.Fori(0, PAIRS // 2) as i:
                for u in (0, 1):
                    b = 2 * i + u
                    turned_low(b + 1, 1 - u)
                    normalise(1, b + 2, u)
                    add_feed_forward(b, u, i)
            for u in (0, 1):
                normalise(2, u, u)
            for b in range(B // 2, B):
                if b + 1 < B:
                    turned_low(b + 1, 1 - b % 2)
                if b + 2 < B:
                    normalise(1, b + 2, b % 2)
                add_feed_forward(b, b % 2, b // 2)
                for item in FIRST[b]:
                    ahead_low(0, *item)
            values(0, 1)

            def experts_low(b, u):
                dve.wait_ge(xT_high[3], b + 1)
                low(xT[:, u, 1, :, :], bank[:, 4 * u, :], xT[:, u, 0, :, :]).then_inc(xT_low[3], 1)

            def choose_experts(b, u):
                s = bank[:, 4 * u + 1, 0:EXPERTS]
                dve.wait_ge(r_mm, b + 1)
                settle()
                v.max(rt[:, u, 0, :], s).then_inc(r_top, 1)
                dve.wait_ge(r_top, b + 1)
                v.tensor_scalar(rs[:, u, 0:1], rt[:, u, 0, 0:1], -1.0, None, ALU.mult).then_inc(r_neg, 1)
                v.match_replace(rl[:, u, 0, :], rt[:, u, 0, :], s, TAKEN).then_inc(r_less, 1)
                dve.wait_ge(r_less, b + 1)
                settle()
                v.max(rt[:, u, 1, :], rl[:, u, 0, :]).then_inc(r_top2, 1)
                dve.wait_ge(r_top2, b + 1)
                settle()
                v.match_replace(rl[:, u, 1, :], rt[:, u, 1, :], rl[:, u, 0, :], TAKEN).then_inc(r_less2, 1)
                dve.wait_ge(r_less2, b + 1)
                dve.wait_ge(r_exp, b + 1)
                v.scalar_tensor_tensor(rk[:, u, :], rl[:, u, 1, :], TAKEN, re[:, u, :],
                                       ALU.is_equal, ALU.mult).then_inc(r_kept, 1)
                dve.wait_ge(r_kept, b + 1)
                v.reduce_sum(rs[:, u, 1:2], rk[:, u, :], AX).then_inc(r_sum, 1)
                dve.wait_ge(r_sum, b + 1)
                v.reciprocal(rs[:, u, 2:3], rs[:, u, 1:2]).then_inc(r_inv, 1)
                dve.wait_ge(r_inv, b + 1)
                v.tensor_scalar(G[:, u, :], rk[:, u, :], rs[:, u, 2:3], None, ALU.mult).then_inc(gate_set, 1)
                dve.wait_ge(gate_set, b + 1)

            def gated(b, u):
                for q in (0, 1):
                    dve.wait_ge(h_mm, 2 * b + q + 1)
                    v.tensor_tensor(hg[u][:, 32 * q:32 * q + 32, :],
                                    bank[:, 4 * u + 2 + q, :].rearrange("p (k r) -> p k r", r=RANK),
                                    G[:, u, 32 * q:32 * q + 32].unsqueeze(2).broadcast_to([P, 32, RANK]),
                                    ALU.mult).then_inc(hg_set, 1)

            def attended(b, u, half):
                m = bank[:, AV_BANK[half], 0:4 * HPG * VW].rearrange("p (h w) -> p h w", w=VW)
                dve.wait_ge(av_mm, GROUPS * b + 4 * half + 4)
                v.reciprocal(iden[:, half, :], m[:, :, DH]).then_inc(inv_den, 1)
                dve.wait_ge(inv_den, 2 * b + half + 1)
                o = att[:, u, half * 256:(half + 1) * 256].rearrange("p (h w) -> p h w", w=DH)
                v.tensor_tensor(o, m[:, :, 0:DH], iden[:, half, :].unsqueeze(2).broadcast_to([P, 4 * HPG, DH]),
                                ALU.mult).then_inc(att_set, 1)

            def attention_low(i, u):
                dve.wait_ge(aT_high, 2 * i + u + 1)
                low(aT[:, u, 1, :, :], bank[:, SPARE, :], aT[:, u, 0, :, :]).then_inc(aT_low, 1)

            def add_attention(i, u):
                b = 2 * i + u
                dve.wait_ge(o_mm, b + 1)
                v.tensor_tensor(X[:, b, :], bank[:, SPARE, :], X[:, b, :], ALU.add).then_inc(x_new[2][u], 1)

            def row_maxima(b, u, banks):
                for n in banks:
                    half, r = n // 4, n % 4
                    dve.wait_ge(score_mm, MAX_BANKS * b + n + 1)
                    v.reduce_max(mx[:, u, :, r, 2 * half:2 * half + 2].rearrange("p e j -> p j e"),
                                 max_bank(u, n).rearrange("p (j e s) -> p j e s", j=2, e=2), AX).then_inc(row_max, 1)

            def maxima_low(b, u):
                dve.wait_ge(mT_high, b + 1)
                v.scalar_tensor_tensor(mT[:, u, 1, :], bank[0:HEADS, TURNED_MAX[u], 0:S], -1.0, mT[:, u, 0, :].bitcast(F32),
                                       ALU.mult, ALU.subtract).then_inc(mT_low, 1)

            def attention(i, ahead):
                row_maxima(2 * i + 1, 1, range(MAX_FIRST))
                if ahead:
                    for u in (0, 1):
                        normalise(2, 2 * i + 2 + u, u)
                for s in range(STEPS):
                    if s in MAX_STEPS:
                        row_maxima(2 * i + 1, 1, range(MAX_FIRST + 2 * s, MAX_FIRST + 2 * s + 2))
                    if s == MAX_TURN:
                        maxima_low(2 * i + 1, 1)
                    if ahead and s in AHEAD:
                        ahead_low(i + 1, *AHEAD[s])
                    if not ahead and s == 2:
                        for u in (0, 1):
                            token_stats(3, u, u)
                    if s in (5, 9, 13):
                        attended(2 * i + s // 13, s // 13, (s - 5) // 4 % 2)
                    if s == 12:
                        attention_low(i, 0)
                    if s == 15:
                        add_attention(i, 0)
                        if not ahead:
                            normalise(3, 0, 0)
                attended(2 * i + 1, 1, 1)
                if not ahead:
                    experts_low(0, 0)
                if ahead:
                    values(i + 1, 1)
                    row_maxima(2 * i + 2, 0, (0, 1))
                attention_low(i, 1)
                if ahead:
                    row_maxima(2 * i + 2, 0, range(2, MAX_BANKS))
                else:
                    normalise(3, 1, 1)
                    choose_experts(0, 0)
                if ahead:
                    maxima_low(2 * i + 2, 0)
                add_attention(i, 1)
                if not ahead:
                    gated(0, 0)
                    experts_low(1, 1)

            row_maxima(0, 0, range(MAX_BANKS))
            maxima_low(0, 0)
            with dve.Fori(0, PAIRS - 1) as i:
                attention(i, True)
            attention(PAIRS - 1, False)

            def turned_gated_low(b, u):
                for q in (0, 1):
                    dve.wait_ge(hT_high, 2 * b + q + 1)
                    low(hT[u][:, 1, 4 * q:4 * q + 4, :], bank[:, 4 * u + q, :], hT[u][:, 0, 4 * q:4 * q + 4, :]).then_inc(hT_low, 1)

            def add_experts(b, u):
                dve.wait_ge(e_mm, b + 1)
                v.tensor_tensor(X[:, b, :], bank[:, 4 * u + 2, :], X[:, b, :], ALU.add).then_inc(x_new[3][u], 1)

            def experts_step(b, u, last_steps=False):
                if not last_steps:
                    token_stats(3, b + 2, u)
                turned_gated_low(b, u)
                if not last_steps:
                    normalise(3, b + 2, u)
                choose_experts(b + 1, 1 - u)
                gated(b + 1, 1 - u)
                if not last_steps:
                    experts_low(b + 2, u)
                add_experts(b, u)

            dve.wait_ge(x_new[2][1], PAIRS + 1)
            with dve.Fori(0, PAIRS - 1) as i:
                for u in (0, 1):
                    experts_step(2 * i + u, u)
            experts_step(B - 2, 0, last_steps=True)
            turned_gated_low(B - 1, 1)
            add_experts(B - 1, 1)

        @block.tensor
        def _(pe):
            t = nc.tensor

            def mm(o, l, r, start=True, stop=True):
                return t.matmul(o, l, r, start=start, stop=stop)

            def mm3(o, l, r, start=True, stop=True):
                mm(o, l[0], r[0], start, False)
                mm(o, l[0], r[1], False, False)
                return mm(o, l[1], r[0], False, stop)

            def transposes(o, src):
                for c in range(C):
                    last = t.transpose(o[:, c * P:(c + 1) * P], src[:, c * P:(c + 1) * P], ident)
                return last

            pe.wait_ge(mats_in, 16)

            def spectra(b, u, i, read=None):
                k, c_in = 4 * u, ctx_s[:, u, :]
                pe.wait_ge(ctx_ld[u], 16 * i + 16)
                if read is not None:
                    pe.wait_ge(spec_prod, read)
                mm(bank[:, k + 3, :], mat["FA"], c_in).then_inc(cyc_mm, 1)
                mm(bank[:, k + 1, :], mat["FL"], c_in).then_inc(half_mm[u], 1)
                pe.wait_ge(normed[0], b + 1)
                mm(bank[:, k + 2, :], mat["FA"], xn[:, u, :]).then_inc(a_mm, 1)

            def correlate(b, u, i):
                pe.wait_ge(x_new[0][u], i + 1)
                pe.wait_ge(corr_prod, 2 * b + 2)
                for c in range(C):
                    cs = slice(c * P, (c + 1) * P)
                    mm(bank[:, 4 * u, cs], spec[u][0][:, cs], mat["G1"], stop=False)
                    last = mm(bank[:, 4 * u, cs], spec[u][1][:, cs], mat["G2"], start=False)
                last.then_inc(corr_mm, 1)

            def weight_spectra(b, u):
                k = 4 * u
                pe.wait_ge(w_built, C * b + C)
                pe.wait_ge(x_spec_out, b + 1)
                for c in range(C):
                    last = t.transpose(bank[:, k + 2, c * P:(c + 1) * P], wts[:, u, c, :], ident)
                last.then_inc(wt_mm, 1)
                pe.wait_ge(cyc_out, 2 * b + 2)
                pe.wait_ge(half_out, 2 * b + 2)
                pe.wait_ge(wt_out, b + 1)
                mm(bank[:, k + 3, :], mat["FA"], wT[:, u, :]).then_inc(we_mm, 1)
                mm(bank[:, k + 1, :], mat["FO"], wT[:, u, :]).then_inc(wo_mm, 1)

            def delayed_sum(b, u):
                for n, name in enumerate(("H1", "H2", "J1", "J2")):
                    pe.wait_ge(spec_prod, 4 * b + n + 1)
                    last = mm(bank[:, 4 * u, :], mat[name], spec[u][n], start=n == 0, stop=n == 3)
                last.then_inc(inv_mm, 1)

            def correlate_step(b, u, i, last_steps=False):
                weight_spectra(b, u)
                correlate(b + 1, 1 - u, i + u)
                if not last_steps:
                    spectra(b + 2, u, i + 1, read=4 * b + 4)
                delayed_sum(b, u)

            for u in (0, 1):
                spectra(u, u, 0)
            pe.wait_ge(rest_in, 32)
            correlate(0, 0, 0)
            with pe.Fori(0, PAIRS - 1) as i:
                for u in (0, 1):
                    correlate_step(2 * i + u, u, i)
            correlate_step(B - 2, 0, PAIRS - 1, last_steps=True)
            pe.wait_ge(lora_in, 16 * 5)
            pe.wait_ge(scaled, 3)

            def low_rank(c):
                mm(bank[:, LORA_BANK[c], :], LA[:, c * P:(c + 1) * P], LB[:]).then_inc(lora_mm, 1)

            for c in range(C - 1):
                low_rank(c)
            weight_spectra(B - 1, 1)
            pe.wait_ge(lora_folded, 1)
            low_rank(C - 1)
            delayed_sum(B - 1, 1)

            def turned(b, u):
                pe.wait_ge(normed[1], b + 1)
                transposes(bank[:, 6 + u, :], xn2[:, u, :]).then_inc(xT_mm[1], 1)

            def feed_forward(b, u, i):
                pe.wait_ge(x_new[1][u], i + 1)
                pe.wait_ge(xT_low[1], b + 1)
                for c in range(C):
                    last = mm3(bank[:, 4 + u, :], [xT2[:, u, w, c, :] for w in (0, 1)],
                               [W0p[:, w, c, :] for w in (0, 1)], c == 0, c == C - 1)
                last.then_inc(y_mm, 1)

            turned(0, 0)
            pe.wait_ge(x_new[0][1], PAIRS + 1)
            pe.wait_ge(w0_low, C)
            def ahead_mm(pair, item, n, after_maxima=None):
                o = input_bank(pair, item, n)
                if item == "x":
                    pe.wait_ge(normed[2], 2 * pair + n + 1)
                    if after_maxima is not None:
                        pe.wait_ge(cT_low, 2 * pair + n + 1)
                    transposes(o, xn[:, n, :]).then_inc(xT_mm[2], 1)
                elif item == "c":
                    pe.wait_ge(ctx_ld[n], 16 * pair + 16 * PAIRS + 16)
                    if after_maxima is not None and n == 1:
                        pe.wait_ge(xT_low[2], 2 * pair + 1)
                    elif after_maxima is not None:
                        pe.wait_ge(mT_low, after_maxima)
                    transposes(o, ctx_s[:, n, :]).then_inc(cT_mm[n], 1)
                elif item == "q":
                    pe.wait_ge(xT_low[2], 2 * pair + 2)
                    if n == 1:
                        pe.wait_ge(cT_low, 2 * pair + 2)
                    for j in (0, 1):
                        js = slice((2 * n + j) * P, (2 * n + j + 1) * P)
                        for c in range(C):
                            last = mm3(o[:, j * 2 * S:(j + 1) * 2 * S], [WQ[:, w, c, js] for w in (0, 1)],
                                       [xT3[:, c, w, :, :] for w in (0, 1)], c == 0, c == C - 1)
                    last.then_inc(q_mm, 1)
                elif item == "k":
                    pe.wait_ge(cT_low, 2 * pair + 2)
                    values_mm(o, 0)
                    for c in range(C):
                        last = mm3(o[:, 0:2 * S], [WK[:, w, c, :] for w in (0, 1)], [cT[:, c, w, :, :] for w in (0, 1)],
                                   c == 0, c == C - 1)
                    last.then_inc(k_mm, 1)
                elif item == "v":
                    pe.wait_ge(q_low, 2 * pair + 2)
                    values_mm(o, 1)

            def values_mm(o, u):
                for c in range(C):
                    last = mm3(o[:, (2 + u) * S:(3 + u) * S], [cT[:, c, w, u, :] for w in (0, 1)],
                               [WV[:, w, c, :] for w in (0, 1)], c == 0, c == C - 1)
                last.then_inc(v_mm, 1)

            with pe.Fori(0, PAIRS // 2) as i:
                for u in (0, 1):
                    turned(2 * i + u + 1, 1 - u)
                    feed_forward(2 * i + u, u, i)
            pe.wait_ge(raw_split, N_ATTN)
            for b in range(B // 2, B):
                if b + 1 < B:
                    turned(b + 1, 1 - b % 2)
                feed_forward(b, b % 2, b // 2)
                for item in FIRST[b]:
                    ahead_mm(0, *item)

            pe.wait_ge(ready_bf, 2)
            pe.wait_ge(ones_set, 6)
            attn_rows = slice(0, STACK)

            def scores_for_max(i, u, banks):
                b = 2 * i + u
                for n in banks:
                    half, r = n // 4, n % 4
                    o = max_bank(u, n)
                    if n == 0:
                        pe.wait_ge(stacked[u], 16 * 6 * i + 16 * 6)
                    if n == 1 and u == 0:
                        pe.wait_ge(v_set, b + 2)
                    if n >= 4:
                        pe.wait_ge(row_max, MAX_BANKS * b + n - (3 if u == 0 or n < 6 else 1))
                    elif u == 1:
                        pe.wait_ge(row_max, MAX_BANKS * b)
                    mm(o, ident_bf[:], never[:, 0, :].unsqueeze(1).broadcast_to([P, 4, S]), stop=False)
                    for jl in (0, 1):
                        j = 2 * half + jl
                        last = mm(o[:, jl * 256:(jl + 1) * 256], qst[0:TOP_ROW, u, r, j * P:(j + 1) * P],
                                  kst[0:TOP_ROW, u, r, :, :], False, jl == 1)
                    last.then_inc(score_mm, 1)

            def turned_maxima(i, u):
                b = 2 * i + u
                if u == 1:
                    pe.wait_ge(x_new[2][1], i + 1)
                pe.wait_ge(row_max, MAX_BANKS * b + MAX_BANKS)
                t.transpose(bank[0:HEADS, TURNED_MAX[u], 0:S],
                            mx[:, u, :, :, :].rearrange("p e r j -> p (e r j)"), ident).then_inc(mT_mm, 1)

            def scores_less_max(i, s):
                u, g = s // GROUPS, s % GROUPS
                o = bank[:, LESS_RING[s % 2], :]
                if g == 0:
                    pe.wait_ge(maxima_in[u], 64 * i + 64)
                if s >= 2:
                    pe.wait_ge(probs, STEPS * i + s - 1)
                else:
                    pe.wait_ge(row_max, MAX_BANKS * (2 * i + 1) + 3 + s)
                mm(o, ident_bf[:], never[:, 1, :].unsqueeze(1).broadcast_to([P, HPG, S]), stop=False)
                mm(o, kst[attn_rows, u, g // 2, g % 2, :], qst[attn_rows, u, g // 2, :], False, True).then_inc(less_mm, 1)

            def attend(i, s):
                u, g = s // GROUPS, s % GROUPS
                if u == 1 and g % 4 == 0:
                    pe.wait_ge(att_set, 4 * i + 1 + g // 4)
                pe.wait_ge(probs, STEPS * i + s + 1)
                for j in range(HPG):
                    at = (g % 4 * HPG + j) * VW
                    last = mm(bank[:, AV_BANK[g // 4], at:at + VW], ET[:, s % 4, j, :], vx[:, u, g, :])
                last.then_inc(av_mm, 1)

            def turned_attention(i, u):
                pe.wait_ge(att_set, 4 * i + 2 * u + 2)
                if u == 0:
                    pe.wait_ge(mT_low, 2 * i + 2)
                else:
                    pe.wait_ge(x_new[2][0], i + 2)
                transposes(bank[:, SPARE, :], att[:, u, :]).then_inc(aT_mm, 1)

            def output_projection(i, u, chunks=range(C)):
                pe.wait_ge(aT_low, 2 * i + u + 1)
                for c in chunks:
                    last = mm3(bank[:, SPARE, :], [aT[:, u, w, c, :] for w in (0, 1)], [WO[:, w, c, :] for w in (0, 1)],
                               c == 0, c == C - 1)
                if C - 1 in chunks:
                    last.then_inc(o_mm, 1)

            def turned_input(b, u):
                pe.wait_ge(normed[3], b + 1)
                transposes(bank[:, 4 * u, :], xn[:, u, :]).then_inc(xT_mm[3], 1)

            def router_mm(b, u):
                pe.wait_ge(xT_low[3], b + 1)
                for c in range(C):
                    last = mm3(bank[:, 4 * u + 1, 0:EXPERTS], [xT[:, u, w, c, :] for w in (0, 1)],
                               [WR[:, w, c, :] for w in (0, 1)], c == 0, c == C - 1)
                last.then_inc(r_mm, 1)

            def experts_in(b, u, i):
                pe.wait_ge(x_new[3][u], i + 1)
                for q in (0, 1):
                    for c in range(C):
                        last = mm3(bank[:, 4 * u + 2 + q, :], [xT[:, u, w, c, :] for w in (0, 1)],
                                   [MA[:, w, c, q * D:(q + 1) * D] for w in (0, 1)], c == 0, c == C - 1)
                    last.then_inc(h_mm, 1)

            def attention(i, ahead):
                scores_for_max(i, 1, range(MAX_FIRST))
                for s in range(STEPS):
                    if s in MAX_STEPS:
                        scores_for_max(i, 1, range(MAX_FIRST + 2 * s, MAX_FIRST + 2 * s + 2))
                    scores_less_max(i, s)
                    if s >= 2:
                        attend(i, s - 2)
                    if s == MAX_TURN:
                        turned_maxima(i, 1)
                    if ahead and s in AHEAD:
                        ahead_mm(i + 1, *AHEAD[s], after_maxima=2 * i + 1)
                    if s == 11:
                        turned_attention(i, 0)
                    if s == 14:
                        output_projection(i, 0)
                attend(i, STEPS - 2)
                attend(i, STEPS - 1)
                if ahead:
                    scores_for_max(i + 1, 0, (0, 1, 2))
                else:
                    turned_input(0, 0)
                turned_attention(i, 1)
                if ahead:
                    scores_for_max(i + 1, 0, (3, 4))
                else:
                    pe.wait_ge(raw_split, N_ATTN + len(staged))
                    router_mm(0, 0)
                output_projection(i, 1, range(C // 2))
                if ahead:
                    scores_for_max(i + 1, 0, range(5, MAX_BANKS))
                    turned_maxima(i + 1, 0)
                output_projection(i, 1, range(C // 2, C))
                if not ahead:
                    experts_in(0, 0, 0)
                    turned_input(1, 1)

            scores_for_max(0, 0, range(MAX_BANKS))
            turned_maxima(0, 0)
            with pe.Fori(0, PAIRS - 1) as i:
                attention(i, True)
            attention(PAIRS - 1, False)

            def turned_gated(b, u):
                hf = hg[u].rearrange("p k r -> p (k r)")
                for q in (0, 1):
                    pe.wait_ge(hg_set, 2 * b + q + 1)
                    transposes(bank[:, 4 * u + q, :], hf[:, q * D:(q + 1) * D]).then_inc(hT_mm, 1)

            def experts_out(b, u):
                for c in range(KC):
                    if c % C == 0:
                        pe.wait_ge(hT_low, 2 * b + c // C + 1)
                    last = mm3(bank[:, 4 * u + 2, :], [hT[u][:, w, c, :] for w in (0, 1)], [MB[:, w, c, :] for w in (0, 1)],
                               c == 0, c == KC - 1)
                last.then_inc(e_mm, 1)

            def experts_step(b, u, i, last_steps=False):
                turned_gated(b, u)
                router_mm(b + 1, 1 - u)
                experts_in(b + 1, 1 - u, i + u)
                if not last_steps:
                    pe.wait_ge(hT_low, 2 * b + 2)
                    turned_input(b + 2, u)
                experts_out(b, u)

            pe.wait_ge(x_new[2][1], PAIRS + 1)
            with pe.Fori(0, PAIRS - 1) as i:
                for u in (0, 1):
                    experts_step(2 * i + u, u, i)
            experts_step(B - 2, 0, PAIRS - 1, last_steps=True)
            turned_gated(B - 1, 1)
            experts_out(B - 1, 1)


def kernel(x, ctx_4096, mask_SxS2_bk0, g_xattn, g_ffn, L0_ffn_lora_A, L0_ffn_lora_B, L0_ffn_W, L0_ffn_bias,
           L0_ffn_lora_weights, L1_xattn_w_q, L1_xattn_w_k, L1_xattn_w_v, L1_xattn_w_out, L1_ffn_A, L1_ffn_B,
           L1_ffn_Wr):
    import concourse.bacc as bacc
    from concourse.bass_utils import run_bass_kernel_spmd

    def rows_by_chunk(w):
        return w.reshape(-1, P, w.shape[-1]).transpose(1, 0, 2)

    asnp = np.asarray
    g_x, g_f = asnp(g_xattn), asnp(g_ffn)
    gates = np.broadcast_to(np.stack([g_x[0], g_f[0], g_x[1], g_f[1]]), (P, 4))
    wq = asnp(L1_xattn_w_q).reshape(GROUPS, HPG, DH, D).transpose(1, 0, 2, 3).reshape(D, D).T
    m = transform_matrices()
    rows, r = np.arange(P) // DH % 2, np.arange(P) - TOP_ROW
    arrays = {
        "x": asnp(x), "ctx": asnp(ctx_4096), "mask": asnp(mask_SxS2_bk0), "mask_t": asnp(mask_SxS2_bk0).T, "gates": gates,
        "w_base": rows_by_chunk(asnp(L0_ffn_W).T),
        "lora_a": asnp(L0_ffn_lora_A).reshape(P, D),
        "lora_b": asnp(L0_ffn_lora_B).transpose(0, 2, 1).reshape(P, D),
        "lora_w": np.repeat(asnp(L0_ffn_lora_weights), P // 8).reshape(P, 1),
        "bias": np.broadcast_to(asnp(L0_ffn_bias), (P, D)),
        "wq": rows_by_chunk(wq), "wk": rows_by_chunk(asnp(L1_xattn_w_k).T), "wv": rows_by_chunk(asnp(L1_xattn_w_v).T),
        "wo": rows_by_chunk(asnp(L1_xattn_w_out).T),
        "moe_a": rows_by_chunk(asnp(L1_ffn_A).reshape(KR, D).T),
        "moe_b": rows_by_chunk(asnp(L1_ffn_B).transpose(0, 2, 1).reshape(KR, D)),
        "w_router": rows_by_chunk(asnp(L1_ffn_Wr).T),
        "mats": np.stack([m[n] for n in MATS], 1).astype(np.float32),
        "parity": np.stack([rows == 0, rows == 1, r // 2 == 0, r // 2 == 1], 1).astype(np.float32),
    }
    nc = bacc.Bacc("TRN2", target_bir_lowering=False, num_devices=1)
    ins, args = {}, []
    for name, a in arrays.items():
        a = np.ascontiguousarray(a)
        ins[f"in_{name}"] = a
        args.append(nc.dram_tensor(f"in_{name}", a.shape, mybir.dt.from_np(a.dtype), kind="ExternalInput").ap())
    out = nc.dram_tensor("out", (B, S, D), F32, kind="ExternalOutput").ap()
    flamingo_kernel(nc, *args, out)
    r = run_bass_kernel_spmd(nc, [ins], core_ids=[0])
    return r.results[0]["out"]
```
